# Optimizing a Trainium2 kernel written in Bass

```python
import numpy as np
import jax
import jax.numpy as jnp

def _softmax(x, axis=-1):
    return jax.nn.softmax(x, axis=axis)

def _gelu(x):
    return jax.nn.gelu(x, approximate=True)

def _silu(x):
    return jax.nn.silu(x)

def _sigmoid(x):
    return jax.nn.sigmoid(x)

def _layernorm(x, axis=-1, eps=1e-05):
    m = jnp.mean(x, axis=axis, keepdims=True)
    v = jnp.var(x, axis=axis, keepdims=True)
    return (x - m) / jnp.sqrt(v + eps)

def _scatter_add(tgt, idx, src, axis=0):
    return tgt.at[idx].add(src)

def _segment_sum(src, seg, n):
    return jax.ops.segment_sum(src, seg, n)
kernel_name = 'mk_xattn_ffn_d1_seqx_r8_16c7c4'

def setup_inputs(seed: int=0):
    np.random.seed(seed)
    _w = jnp.asarray

    def _rec_inputs():
        import jax
        import jax.numpy as jnp
        _rk = jax.random.key(seed)
        x = 2.818e-05 + 1 * jax.random.normal(jax.random.fold_in(_rk, 1), (4, 256, 256), jnp.float32)
        _lenS = 256 - jax.random.randint(jax.random.fold_in(_rk, 7), (4,), 0, max(1, 256 // 4) + 1, jnp.int32)
        _lenS2 = 256 - jax.random.randint(jax.random.fold_in(_rk, 8), (4,), 0, max(1, 256 // 4) + 1, jnp.int32)
        _ctx_1024P = jax.random.normal(jax.random.fold_in(_rk, 11), (4, 16, 128), jnp.float32)
        _ctx_1024c = jax.random.dirichlet(jax.random.fold_in(_rk, 511), 0.3 * jnp.ones((16,), jnp.float32), (4, 256))
        _ctx_1024t = jnp.einsum('bsk,bkd->bsd', _ctx_1024c, _ctx_1024P)
        _ctx_1024t = _ctx_1024t * jax.lax.rsqrt(jnp.mean(jnp.square(_ctx_1024t)) + 1e-12) * 0.953939
        ctx_1024 = 7.22013e-05 + 1.00017 * (_ctx_1024t + 0.3 * jax.random.normal(jax.random.fold_in(_rk, 611), (4, 256, 128), jnp.float32))
        return (x, ctx_1024)
    x, ctx_1024 = _rec_inputs()

    def _L0_xattn_setup():
        import jax, jax.numpy as jnp
        import numpy as np
        B_, L_, D_MODEL = (4, 256, 128)
        D_STATE, D_CONV, EXPAND = (16, 4, 2)
        D_INNER = EXPAND * D_MODEL
        DT_RANK = (D_MODEL + 15) // 16

        def silu(x):
            return x * jax.nn.sigmoid(x)
        key = jax.random.key(seed)
        ks = jax.random.split(key, 10)
        f32 = jnp.float32
        hidden_states = jax.random.normal(ks[0], (B_, L_, D_MODEL), dtype=f32)
        z = jax.random.normal(ks[1], (B_, D_INNER, L_), dtype=f32)
        in_proj_w = jax.random.normal(ks[2], (D_INNER, D_MODEL), dtype=f32) * 0.02
        conv_w = jax.random.normal(ks[3], (D_INNER, 1, D_CONV), dtype=f32) * 0.1
        conv_b = jax.random.normal(ks[4], (D_INNER,), dtype=f32) * 0.02
        x_proj_w = jax.random.normal(ks[5], (DT_RANK + 2 * D_STATE, D_INNER), dtype=f32) * 0.02
        dt_proj_w = jax.random.uniform(ks[6], (D_INNER, DT_RANK), dtype=f32, minval=-DT_RANK ** (-0.5), maxval=DT_RANK ** (-0.5))
        dt = jnp.exp(jax.random.uniform(ks[7], (D_INNER,), dtype=f32, minval=np.log(0.001), maxval=np.log(0.1)))
        dt_proj_b = jnp.log(jnp.expm1(dt))
        A_log = jnp.log(jnp.broadcast_to(jnp.arange(1, D_STATE + 1, dtype=f32), (D_INNER, D_STATE)))
        D = jnp.ones((D_INNER,), f32)
        return {'hidden_states': hidden_states, 'z': z, 'in_proj_w': in_proj_w, 'conv_w': conv_w, 'conv_b': conv_b, 'x_proj_w': x_proj_w, 'dt_proj_w': dt_proj_w, 'dt_proj_b': dt_proj_b, 'A_log': A_log, 'D': D}
    _L0_xattn_all = _L0_xattn_setup()
    _L0_xattn_in = {k: v for k, v in _L0_xattn_all.items() if k in ('in_proj_w', 'conv_w', 'conv_b', 'x_proj_w', 'dt_proj_w', 'dt_proj_b', 'A_log', 'D')}
    del _L0_xattn_all

    def _L0_ffn_setup():
        import jax, jax.numpy as jnp
        import numpy as np
        B, S, H = (1, 128, 256)
        F = 128
        E = 16
        K = 2
        NS = 1
        ROUTE_SCALE = 1.0
        key = jax.random.key(seed)
        ks = jax.random.split(key, 8)

        def w(k, shape, fan_in):
            return jax.random.normal(k, shape, jnp.float32) * fan_in ** (-0.5)
        return {'hidden_states': jax.random.normal(ks[0], (B, S, H), jnp.float32), 'gate_w': w(ks[1], (H, E), H), 'expert_bias': jnp.zeros((E,), jnp.float32), 'shared_gate_w': w(ks[2], (H, F * NS), H), 'shared_up_w': w(ks[3], (H, F * NS), H), 'shared_down_w': w(ks[4], (F * NS, H), F * NS), 'experts_gate_up': w(ks[5], (E, H, 2 * F), H), 'experts_down': w(ks[6], (E, F, H), F)}
    _L0_ffn_all = _L0_ffn_setup()
    _L0_ffn_in = {k: v for k, v in _L0_ffn_all.items() if k in ('gate_w', 'expert_bias', 'shared_gate_w', 'shared_up_w', 'shared_down_w', 'experts_gate_up', 'experts_down')}
    del _L0_ffn_all
    return {'x': x, 'ctx_1024': ctx_1024, 'L0_xattn_in_proj_w': _L0_xattn_in['in_proj_w'], 'L0_xattn_conv_w': _L0_xattn_in['conv_w'], 'L0_xattn_conv_b': _L0_xattn_in['conv_b'], 'L0_xattn_x_proj_w': _L0_xattn_in['x_proj_w'], 'L0_xattn_dt_proj_w': _L0_xattn_in['dt_proj_w'], 'L0_xattn_dt_proj_b': _L0_xattn_in['dt_proj_b'], 'L0_xattn_A_log': _L0_xattn_in['A_log'], 'L0_xattn_D': _L0_xattn_in['D'], 'L0_ffn_gate_w': _L0_ffn_in['gate_w'], 'L0_ffn_expert_bias': _L0_ffn_in['expert_bias'], 'L0_ffn_shared_gate_w': _L0_ffn_in['shared_gate_w'], 'L0_ffn_shared_up_w': _L0_ffn_in['shared_up_w'], 'L0_ffn_shared_down_w': _L0_ffn_in['shared_down_w'], 'L0_ffn_experts_gate_up': _L0_ffn_in['experts_gate_up'], 'L0_ffn_experts_down': _L0_ffn_in['experts_down']}

def reference(x, ctx_1024, L0_xattn_in_proj_w, L0_xattn_conv_w, L0_xattn_conv_b, L0_xattn_x_proj_w, L0_xattn_dt_proj_w, L0_xattn_dt_proj_b, L0_xattn_A_log, L0_xattn_D, L0_ffn_gate_w, L0_ffn_expert_bias, L0_ffn_shared_gate_w, L0_ffn_shared_up_w, L0_ffn_shared_down_w, L0_ffn_experts_gate_up, L0_ffn_experts_down):
    import jax
    import jax.numpy as jnp

    def _L0_xattn_ref(hidden_states, z, in_proj_w, conv_w, conv_b, x_proj_w, dt_proj_w, dt_proj_b, A_log, D):
        import jax, jax.numpy as jnp
        import numpy as np
        B_, L_, D_MODEL = (4, 256, 128)
        D_STATE, D_CONV, EXPAND = (16, 4, 2)
        D_INNER = EXPAND * D_MODEL
        DT_RANK = (D_MODEL + 15) // 16

        def silu(x):
            return x * jax.nn.sigmoid(x)
        Bsz, L, _ = hidden_states.shape
        d_inner, _, d_conv = conv_w.shape
        dt_rank = dt_proj_w.shape[1]
        d_state = A_log.shape[1]
        x = jnp.einsum('bld,ed->bel', hidden_states, in_proj_w)
        xc = jax.lax.conv_general_dilated(x, conv_w, window_strides=(1,), padding=[(d_conv - 1, 0)], feature_group_count=d_inner, dimension_numbers=('NCH', 'OIH', 'NCH'))
        x = silu(xc + conv_b[None, :, None])
        x_dbl = jnp.einsum('bdl,ed->bel', x, x_proj_w)
        dt_low, Bm, Cm = jnp.split(x_dbl, [dt_rank, dt_rank + d_state], axis=1)
        dt = jnp.einsum('brl,dr->bdl', dt_low, dt_proj_w)
        dt = jax.nn.softplus(dt + dt_proj_b[None, :, None])
        A = -jnp.exp(A_log)
        dt_t = jnp.moveaxis(dt, -1, 0)
        B_t = jnp.moveaxis(Bm, -1, 0)
        C_t = jnp.moveaxis(Cm, -1, 0)
        u_t = jnp.moveaxis(x, -1, 0)

        def step(state, inp):
            d, b, c, u = inp
            dA = jnp.exp(d[..., None] * A)
            state = state * dA + (d * u)[..., None] * b[:, None, :]
            y = jnp.einsum('bdn,bn->bd', state, c)
            return (state, y)
        state0 = jnp.zeros((Bsz, d_inner, d_state), x.dtype)
        _, ys = jax.lax.scan(step, state0, (dt_t, B_t, C_t, u_t))
        y = jnp.moveaxis(ys, 0, 2)
        y = y + D[None, :, None] * x
        y = y * silu(z)
        return jnp.swapaxes(y, 1, 2)

    def _L0_ffn_ref(hidden_states, gate_w, expert_bias, shared_gate_w, shared_up_w, shared_down_w, experts_gate_up, experts_down):
        import jax, jax.numpy as jnp
        import numpy as np
        B, S, H = (1, 128, 256)
        F = 128
        E = 16
        K = 2
        NS = 1
        ROUTE_SCALE = 1.0
        b, s, h = hidden_states.shape
        x = hidden_states.reshape(-1, h)
        T = x.shape[0]
        router_logits = (x @ gate_w).astype(jnp.float32)
        scores = jax.nn.sigmoid(router_logits)
        _, selected = jax.lax.top_k(scores + expert_bias[None, :], K)
        top_scores = jnp.take_along_axis(scores, selected, axis=1)
        top_scores = top_scores / (top_scores.sum(-1, keepdims=True) + 1e-20)
        top_scores = top_scores * ROUTE_SCALE
        shared = jax.nn.silu(x @ shared_gate_w) * (x @ shared_up_w) @ shared_down_w
        comb = jnp.zeros((T, E), jnp.float32).at[jnp.arange(T)[:, None], selected].add(top_scores)
        routed = jnp.zeros_like(x)
        for e in range(E):
            gu = x @ experts_gate_up[e]
            g, u = jnp.split(gu, 2, axis=-1)
            routed = routed + comb[:, e:e + 1] * (jax.nn.silu(g) * u @ experts_down[e])
        return (shared + routed).reshape(b, s, h)
    x = x + _L0_xattn_ref(ctx_1024, _layernorm(x, axis=-1), L0_xattn_in_proj_w, L0_xattn_conv_w, L0_xattn_conv_b, L0_xattn_x_proj_w, L0_xattn_dt_proj_w, L0_xattn_dt_proj_b, L0_xattn_A_log, L0_xattn_D)
    x = x + _L0_ffn_ref(_layernorm(x, axis=-1), L0_ffn_gate_w, L0_ffn_expert_bias, L0_ffn_shared_gate_w, L0_ffn_shared_up_w, L0_ffn_shared_down_w, L0_ffn_experts_gate_up, L0_ffn_experts_down)
    return x

_drawn_inputs = setup_inputs


def setup_inputs(seed=0):
    import zlib

    import numpy as np

    out = dict(_drawn_inputs(seed))
    spreads = {'L0_xattn_D': (1.0, 0.6), 'L0_ffn_expert_bias': (0.0, 0.1)}
    factors = {'L0_xattn_x_proj_w': 8.0,
     'L0_xattn_dt_proj_w': 8.0,
     'L0_xattn_dt_proj_b': 8.0,
     'L0_xattn_A_log': 8.0}
    for name, (base, spread) in spreads.items():
        noise = np.random.default_rng([zlib.crc32(name.encode()), seed]).standard_normal(out[name].shape)
        drawn = base * np.exp(spread * noise) if base else spread * noise
        out[name] = jnp.asarray(drawn.astype(out[name].dtype))
    for name, factor in factors.items():
        out[name] = (out[name] * factor).astype(out[name].dtype)
    return out
```

```python
from contextlib import ExitStack

import concourse.bass as bass
from concourse import mybir

ALU = mybir.AluOpType
ACT = mybir.ActivationFunctionType
F32 = mybir.dt.float32
BF16 = mybir.dt.bfloat16
U32 = mybir.dt.uint32
AX_X = mybir.AxisListType.X

P = 128
ATANH = (2.0000000012778267, 0.6666639578183403, 0.4002308285536912, 0.27970779753899433, 0.2818452560443701)


def block_kernel(nc, x, ctx_in, in_proj_w, conv_w, conv_b, x_proj_w, dt_proj_w, dt_proj_b, A_log, D,
                 gate_w, expert_bias, shared_gate_w, shared_up_w, shared_down_w, experts_gate_up,
                 experts_down, out):
    B, L, H = x.shape
    DM = ctx_in.shape[2]
    DI, NS = A_log.shape
    R = dt_proj_w.shape[1]
    K = conv_w.shape[2]
    E = gate_w.shape[1]
    F = shared_gate_w.shape[1]
    HB = DI // P
    LB = L // P
    NT = B * LB
    BH = 2
    TH = B // BH
    C = BH * L
    NBC = 2 * NS
    assert C == 512 and DM == P and F == P and HB == 2 and LB == 2 and H == HB * P and NBC == 32
    EPS = 1e-5

    with ExitStack() as stack:
        def sb(name, shape, dt=F32):
            return stack.enter_context(nc.sbuf_tensor(name, shape, dt))

        def sem(name):
            return stack.enter_context(nc.semaphore(name))

        bank = [stack.enter_context(nc.psum_tensor(f"bank{i}", [P, 512], F32)) for i in range(8)]

        x_sb = sb("x_sb", [P, B, LB, H])
        ctx_sb = sb("ctx_sb", [P, B, LB, DM])
        inw_sb = sb("inw_sb", [P, HB, DM])
        cw_sb = sb("cw_sb", [P, HB, K])
        vec_rows = sb("vec_rows", [3 * HB, P])
        vec_sb = sb("vec_sb", [P, 3, HB])
        xp_sb = sb("xp_sb", [R + NBC, DI])
        dp_sb = sb("dp_sb", [P, HB, R])
        al_sb = sb("al_sb", [P, HB, NS])
        gatew_sb = sb("gatew_sb", [P, HB, E])
        bias_sb = sb("bias_sb", [P, E])
        gu_sb = sb("gu_sb", [P, E + 1, HB, 2 * F])
        dn_sb = sb("dn_sb", [P, E + 1, H])

        ident = sb("ident", [P, P])
        rowsel = sb("rowsel", [3 * NBC, NBC, P], BF16)
        rowsel1 = sb("rowsel1", [3 * NBC, NBC])
        minus_half = sb("minus_half", [P, NT])
        expert_no = sb("expert_no", [P, E])

        ctxT = sb("ctxT", [P, B, K - 1 + L])
        wk = sb("wk", [P, HB, K, DM])
        wkT = sb("wkT", [P, HB, K, P])
        bcT = sb("bcT", [P, HB, 3, NBC])
        dlT = sb("dlT", [P, HB, R])
        dpT = sb("dpT", [R, HB, P])
        A_sb = sb("A_sb", [P, HB, NS])
        u_sb = sb("u_sb", [P, TH, HB, C])
        du_sb = sb("du_sb", [P, TH, HB, C])
        dt_sb = sb("dt_sb", [P, TH, HB, C])
        dtu_sb = sb("dtu_sb", [P, TH, HB, C])
        zs_sb = sb("zs_sb", [P, TH, HB, C])
        bc_hi = sb("bc_hi", [3 * NBC, TH, C], BF16)
        bc_res = sb("bc_res", [3 * NBC, TH, C])
        dl_sb = sb("dl_sb", [R, TH, C])
        sp = {n: sb(f"sp_{n}", [P, TH, HB, C]) for n in ("x", "e", "s", "t", "v")}
        st6 = sb("st6", [P, NT, 6])
        mv = sb("mv", [P, NT, 2])
        ve = sb("ve", [P, NT])
        rstd = sb("rstd", [P, NT])
        nmr = sb("nmr", [P, NT])
        brep = sb("brep", [P, C])
        dbu = sb("dbu", [P, HB, C])
        hst = sb("hst", [P, HB, C])
        hc = sb("hc", [P, HB, C])
        yz = sb("yz", [P, HB, C])

        xh = sp["e"][:].rearrange("p a h c -> p (a h c)").rearrange("p (t d) -> p t d", t=NT)
        xhT = sp["s"][:].rearrange("p a h c -> p (a h c)").rearrange("p (k t q) -> p k t q", k=HB, t=NT)
        score = sb("score", [P, NT, E])
        biased = sb("biased", [P, NT, E])
        top = sb("top", [P, NT, 8])
        topi = sb("topi", [P, NT, 8], U32)
        topf = sb("topf", [P, NT, 2])
        m0 = sb("m0", [P, NT, E])
        m1 = sb("m1", [P, NT, E])
        wsum = sb("wsum", [P, NT])
        winv = sb("winv", [P, NT])
        comb = sb("comb", [P, NT, E + 1])
        sg = sb("sg", [P, 2, F])
        hm = sb("hm", [P, 2, F])
        hT = sb("hT", [P, 2, P])
        o_sb = sp["t"][:].rearrange("p a h c -> p (a h c)").rearrange("p (t d) -> p t d", t=NT)

        in_small = sem("in_small")
        in_ctx = sem("in_ctx")
        in_w = sem("in_w")
        in_x = sem("in_x")
        in_ffn = sem("in_ffn")
        out_done = sem("out_done")
        consts = sem("consts")
        consts2 = sem("consts2")
        pads = sem("pads")
        wk_scaled = sem("wk_scaled")
        small_T = sem("small_T")
        ctx_T = sem("ctx_T")
        wk_T = sem("wk_T")
        small_c = sem("small_c")
        ctx_c = sem("ctx_c")
        wk_c = sem("wk_c")
        conv_done = sem("conv_done")
        u_ready = sem("u_ready")
        dl_done = sem("dl_done")
        bc_done = sem("bc_done")
        dl_c = sem("dl_c")
        bc_free = sem("bc_free")
        dtp_done = sem("dtp_done")
        spx = sem("spx")
        sp_act = sem("sp_act")
        sp_dve = sem("sp_dve")
        dtu_ready = sem("dtu_ready")
        du_ready = sem("du_ready")
        split_act = sem("split_act")
        split_dve = sem("split_dve")
        dchain = sem("dchain")
        decay_zeroed = sem("decay_zeroed")
        route = sem("route")
        var_ready = sem("var_ready")
        rstd_ready = sem("rstd_ready")
        nmr_ready = sem("nmr_ready")
        z_ready = sem("z_ready")
        a_ready = sem("a_ready")
        brep_made = sem("brep_made")
        brep_copied = sem("brep_copied")
        crep_made = sem("crep_made")
        decay_ready = sem("decay_ready")
        dbu_ready = sem("dbu_ready")
        scanned = sem("scanned")
        hc_ready = sem("hc_ready")
        summed = sem("summed")
        yz_ready = sem("yz_ready")
        yz_T = sem("yz_T")
        x1_ready = sem("x1_ready")
        xh_ready = sem("xh_ready")
        xh_T = sem("xh_T")
        xh_c = sem("xh_c")
        logits = sem("logits")
        scored = sem("scored")
        comb_ready = sem("comb_ready")
        gu_made = sem("gu_made")
        silu_done = sem("silu_done")
        hm_ready = sem("hm_ready")
        h_T = sem("h_T")
        hT_ready = sem("hT_ready")
        down_done = sem("down_done")
        o_ready = sem("o_ready")

        y_ps = [bank[0], bank[1]]
        b_ps, c_ps = bank[2], bank[3]
        yT_ps = [bank[4], bank[7]]
        decay_ps = [bank[5], bank[6]]

        def dtp_bank(k):
            return bank[(5 + k) % 8][:]

        block = stack.enter_context(nc.Block())

        @block.sync
        def _(sp_):
            sp_.dma_start(ctx_sb[:], ctx_in.rearrange("b (t p) d -> p b t d", p=P)).then_inc(in_ctx, 16)
            sp_.dma_start(x_sb[:], x.rearrange("b (t p) d -> p b t d", p=P)).then_inc(in_x, 16)
            sp_.dma_start(gu_sb[:, 0, :, 0:F], shared_gate_w.rearrange("(k p) f -> p k f", p=P)).then_inc(in_ffn, 16)
            sp_.dma_start(gu_sb[:, 0, :, F:2 * F], shared_up_w.rearrange("(k p) f -> p k f", p=P)).then_inc(in_ffn, 16)
            sp_.dma_start(dn_sb[:, 0, :], shared_down_w).then_inc(in_ffn, 16)
            for k in range(HB):
                sp_.dma_start(gu_sb[:, 1:, k, :],
                              experts_gate_up[:, k * P:(k + 1) * P, :].rearrange("e p f -> p e f")).then_inc(in_ffn, 16)
            sp_.dma_start(dn_sb[:, 1:, :], experts_down.rearrange("e p h -> p e h")).then_inc(in_ffn, 16)
            for t in range(NT):
                sp_.wait_ge(o_ready, t + 1)
                sp_.dma_start(out[t // LB, (t % LB) * P:(t % LB + 1) * P, :], o_sb[:, t, :]).then_inc(out_done, 16)
            sp_.wait_ge(out_done, 16 * NT)

        @block.gpsimd
        def _(pool):
            nc.gpsimd.memset(ident[:], 0.0).then_inc(consts2, 1)
            nc.gpsimd.memset(ctxT[:], 0.0).then_inc(pads, 1)
            pool.wait_ge(consts2, 1)
            nc.gpsimd.affine_select(out=ident[:], in_=ident[:], compare_op=ALU.not_equal, fill=1.0, base=0,
                                    pattern=[[-1, P]], channel_multiplier=1).then_inc(consts, 1)
            pool.wait_ge(consts, 1)
            idn = [ident[0:3 * NBC, q * NBC:(q + 1) * NBC] for q in range(3)]
            nc.gpsimd.tensor_tensor(rowsel1[:], idn[0], idn[1], ALU.add).then_inc(consts, 1)
            pool.wait_ge(consts, 2)
            nc.gpsimd.tensor_tensor(rowsel1[:], rowsel1[:], idn[2], ALU.add).then_inc(consts, 1)
            nc.gpsimd.memset(minus_half[:], -0.5).then_inc(consts, 1)
            nc.gpsimd.iota(expert_no[:], [[1, E]], base=0, channel_multiplier=0,
                           allow_small_or_imprecise_dtypes=True).then_inc(consts, 1)
            pool.wait_ge(consts, 5)
            nc.gpsimd.tensor_copy(rowsel[:], rowsel1[:].unsqueeze(2).to_broadcast([3 * NBC, NBC, P])).then_inc(consts, 1)
            pool.wait_ge(var_ready, 1)
            nc.gpsimd.tensor_tensor(rstd[:], ve[:], minus_half[:], ALU.pow).then_inc(rstd_ready, 1)
            for th in range(TH):
                for h in range(HB):
                    k = th * HB + h
                    pool.wait_ge(u_ready, k + 1)
                    nc.gpsimd.tensor_scalar(du_sb[:, th, h, :], u_sb[:, th, h, :], vec_sb[:, 2, h:h + 1], None,
                                            ALU.mult).then_inc(du_ready, 1)
            for th in range(TH):
                for h in range(HB):
                    pool.wait_ge(sp_dve, 9 * (th * HB + h) + 9)
                    nc.gpsimd.tensor_tensor(dtu_sb[:, th, h, :], dt_sb[:, th, h, :], u_sb[:, th, h, :],
                                            ALU.mult).then_inc(dtu_ready, 1)

            def drive(th, j):
                pool.wait_ge(brep_copied, j + 1)
                for h in range(HB):
                    if not (isinstance(j, int) and j == 0):
                        pool.wait_ge(scanned, HB * j - HB + h + 1)
                    nc.gpsimd.tensor_tensor(dbu[:, h, :], dtu_sb[:, th, h, :], brep[:], ALU.mult).then_inc(dbu_ready, 1)

            for th in range(TH):
                pool.wait_ge(dtu_ready, (th + 1) * HB)
                drive(th, th * NS)
                with pool.Fori(1, NS) as n:
                    drive(th, n + th * NS)
            pool.wait_ge(var_ready, 2)
            nc.gpsimd.tensor_tensor(rstd[:], ve[:], minus_half[:], ALU.pow).then_inc(rstd_ready, 1)

        @block.scalar
        def _(act):
            act.dma_start(inw_sb[:], in_proj_w.rearrange("(h p) d -> p h d", p=P)).then_inc(in_w, 16)
            act.dma_start(cw_sb[:], conv_w.rearrange("(h p) o k -> p h (o k)", p=P)).then_inc(in_w, 16)
            act.dma_start(xp_sb[:], x_proj_w).then_inc(in_small, 16)
            act.dma_start(dp_sb[:], dt_proj_w.rearrange("(h p) r -> p h r", p=P)).then_inc(in_small, 16)
            for i, v in enumerate((conv_b, dt_proj_b, D)):
                act.dma_start(vec_rows[i * HB:(i + 1) * HB, :], v.rearrange("(h p) -> h p", p=P)).then_inc(in_small, 16)
            act.dma_start(al_sb[:], A_log.rearrange("(h p) n -> p h n", p=P)).then_inc(in_small, 16)
            act.dma_start(gatew_sb[:], gate_w.rearrange("(k p) e -> p k e", p=P)).then_inc(in_small, 16)
            act.dma_start(bias_sb[:], expert_bias.partition_broadcast(P)).then_inc(in_small, 16)
            act.wait_ge(pads, 1)
            for th in range(TH):
                act.wait_ge(ctx_T, th + 1)
                nc.scalar.copy(ctxT[:, th * BH:(th + 1) * BH, K - 1:],
                               bank[th][:].rearrange("p (b l) -> p b l", b=BH)).then_inc(ctx_c, 1)
            act.wait_ge(small_c, 3 * HB + 1)
            for k in range(TH * HB):
                th, h = divmod(k, HB)
                act.wait_ge(conv_done, k + 1)
                nc.scalar.activation(u_sb[:, th, h, :], bank[(5 + k) % 8][:], ACT.Silu,
                                     bias=vec_sb[:, 0, h:h + 1]).then_inc(u_ready, 1)
            act.wait_ge(nmr_ready, 1)
            for b in range(B):
                for h in range(HB):
                    t = b * HB + h
                    nc.scalar.activation(zs_sb[:, b // BH, h, (b % BH) * L:(b % BH + 1) * L], x_sb[:, b, h, :],
                                         ACT.Silu, bias=nmr[:, t:t + 1], scale=rstd[:, t:t + 1]).then_inc(z_ready, 1)
            nc.scalar.activation(A_sb[:], al_sb[:], ACT.Exp).then_inc(a_ready, 1)

            for k in range(TH * HB):
                th, h = divmod(k, HB)
                act.wait_ge(spx, k + 1)
                nc.scalar.activation(sp["e"][:, th, h, :], sp["x"][:, th, h, :], ACT.Abs).then_inc(sp_act, 1)
                act.wait_ge(sp_act, 3 * k + 1)
                nc.scalar.activation(sp["e"][:, th, h, :], sp["e"][:, th, h, :], ACT.Exp, scale=-1.0).then_inc(sp_act, 1)
                act.wait_ge(sp_dve, 9 * k + 3)
                nc.scalar.activation(sp["t"][:, th, h, :], sp["s"][:, th, h, :], ACT.Square).then_inc(sp_act, 1)

            def decay(th, j, n):
                first = isinstance(j, int) and j == 0
                for h in range(HB):
                    if not first:
                        act.wait_ge(scanned, HB * j - HB + h + 1)
                    v = decay_ps[h][:].rearrange("p (b l) -> p b l", b=BH)[:, :, 1:]
                    s = dt_sb[:, th, h, :].rearrange("p (b l) -> p b l", b=BH)[:, :, 1:]
                    nc.scalar.activation(v, s, ACT.Exp, scale=A_sb[:, h, bass.ds(n, 1)] if not isinstance(n, int)
                                         else A_sb[:, h, n:n + 1]).then_inc(decay_ready, 1)
                act.wait_ge(brep_made, j + 1)
                if not first:
                    act.wait_ge(dbu_ready, HB * j)
                nc.scalar.copy(brep[:], b_ps[:]).then_inc(brep_copied, 1)

            act.wait_ge(a_ready, 2)
            act.wait_ge(decay_zeroed, HB)
            for th in range(TH):
                act.wait_ge(sp_dve, 9 * (th + 1) * HB)
                decay(th, th * NS, 0)
                with act.Fori(1, NS) as n:
                    decay(th, n + th * NS, n)

            for i in range(4):
                act.wait_ge(xh_T, i + 1)
                nc.scalar.copy(xhT.rearrange("p k t q -> p (k t q)")[:, i * 512:(i + 1) * 512], bank[i][:]).then_inc(xh_c, 1)
            act.wait_ge(logits, 1)
            nc.scalar.activation(score[:].rearrange("p t e -> p (t e)"), bank[4][:, 0:NT * E], ACT.Sigmoid).then_inc(scored, 1)

            def gate(s0, t):
                s = s0 + t
                early = isinstance(s, int) and s < 2
                act.wait_ge(gu_made, s + 1)
                if not early:
                    act.wait_ge(hm_ready, s - 1)
                nc.scalar.activation(sg[:, t % 2, :], bank[4 + t % 2][:, 0:F], ACT.Silu).then_inc(silu_done, 1)

            def move_hT(s0, t):
                s = s0 + t
                early = isinstance(s, int) and s < 2
                act.wait_ge(h_T, s + 1)
                if not early:
                    act.wait_ge(down_done, s - 1)
                nc.scalar.copy(hT[:, t % 2, :], bank[6 + t % 2][:, 0:P]).then_inc(hT_ready, 1)

            for t in range(NT):
                gate(0, t)
                if t >= 1:
                    move_hT(0, t - 1)
            with act.Fori(1, E + 1) as e:
                for t in range(NT):
                    gate(e * NT, t)
                    move_hT(e * NT, t - 1)
            move_hT((E + 1) * NT, -1)

        @block.vector
        def _(dve):
            dve.wait_ge(in_w, 32)
            for h in range(HB):
                for k in range(K):
                    nc.vector.tensor_scalar(wk[:, h, k, :], inw_sb[:, h, :], cw_sb[:, h, k:k + 1], None,
                                            ALU.mult).then_inc(wk_scaled, 1)
            dve.wait_ge(small_T, 1)
            for h in range(HB):
                src = bank[4][:, h * (R + NBC):(h + 1) * (R + NBC)]
                nc.vector.tensor_copy(dlT[:, h, :], src[:, 0:R]).then_inc(small_c, 1)
                nc.vector.tensor_copy(bcT[:, h, :, :], src[:, R:].unsqueeze(1).to_broadcast([P, 3, NBC])).then_inc(small_c, 1)
                nc.vector.tensor_copy(dpT[:, h, :], bank[4][0:R, 128 + h * P:128 + (h + 1) * P]).then_inc(small_c, 1)
            nc.vector.tensor_copy(vec_sb[:].rearrange("p v h -> p (v h)"), bank[4][:, 384:384 + 3 * HB]).then_inc(small_c, 1)
            for h in range(HB):
                dve.wait_ge(wk_T, h + 1)
                nc.vector.tensor_copy(wkT[:, h, :, :], bank[2 + h][:].rearrange("p (k q) -> p k q", k=K)).then_inc(wk_c, 1)
            dve.wait_ge(in_x, 16)

            def stats(phase):
                for t in range(NT):
                    nc.vector.bn_stats(st6[:, t, :], x_sb[:, t // LB, t % LB, :]).then_inc(dchain, 1)
                dve.wait_ge(dchain, phase * 2 * NT + NT)
                for t in range(NT):
                    nc.vector.bn_aggr(mv[:, t, :], st6[:, t, :]).then_inc(dchain, 1)
                dve.wait_ge(dchain, phase * 2 * NT + 2 * NT)
                nc.vector.tensor_scalar(ve[:], mv[:, :, 1], EPS, None, ALU.add).then_inc(var_ready, 1)
                dve.wait_ge(rstd_ready, phase + 1)
            stats(0)
            nc.vector.scalar_tensor_tensor(out=nmr[:], in0=mv[:, :, 0], scalar=-1.0, in1=rstd[:],
                                           op0=ALU.mult, op1=ALU.mult).then_inc(nmr_ready, 1)
            dve.wait_ge(a_ready, 1)
            nc.vector.tensor_scalar(A_sb[:], A_sb[:], -1.0, None, ALU.mult).then_inc(a_ready, 1)

            for th in range(TH):
                dve.wait_ge(bc_done, th + 1)
                X = bank[2 + th][0:3 * NBC, :]
                hi = bc_hi[:, th, :]
                res = bc_res[:, th, :]
                c = 5 * th
                nc.vector.tensor_copy(hi, X).then_inc(split_dve, 1)
                dve.wait_ge(split_dve, c + 1)
                nc.vector.tensor_tensor(res, X, hi, ALU.subtract).then_inc(split_dve, 1)
                dve.wait_ge(split_dve, c + 2)
                for q in (1, 2):
                    rows = slice(q * NBC, (q + 1) * NBC)
                    nc.vector.tensor_copy(bc_hi[rows, th, :], bc_res[rows, th, :]).then_inc(split_dve, 1)
                dve.wait_ge(split_dve, c + 4)
                nc.vector.tensor_tensor(bc_hi[rows, th, :], bc_res[rows, th, :], bc_hi[rows, th, :],
                                        ALU.subtract).then_inc(split_dve, 1)
                dve.wait_ge(dl_done, th + 1)
                nc.vector.tensor_copy(dl_sb[:, th, :], bank[4][0:R, :] if th == 0 else bank[1][0:R, :]).then_inc(dl_c, 1)
                for h in range(HB):
                    k = th * HB + h
                    c = 9 * k
                    e, s, t, v, xx = (sp[n][:, th, h, :] for n in ("e", "s", "t", "v", "x"))
                    dve.wait_ge(dtp_done, k + 1)
                    nc.vector.tensor_scalar(xx, dtp_bank(k), vec_sb[:, 1, h:h + 1], None,
                                            ALU.add).then_inc(spx, 1)
                    dve.wait_ge(sp_act, 3 * k + 2)
                    nc.vector.tensor_scalar(v, e, 2.0, None, ALU.add).then_inc(sp_dve, 1)
                    dve.wait_ge(sp_dve, c + 1)
                    nc.vector.reciprocal(v, v).then_inc(sp_dve, 1)
                    dve.wait_ge(sp_dve, c + 2)
                    nc.vector.tensor_tensor(s, e, v, ALU.mult).then_inc(sp_dve, 1)
                    dve.wait_ge(sp_act, 3 * k + 3)
                    nc.vector.tensor_scalar(v, t, ATANH[4], ATANH[3], ALU.mult, ALU.add).then_inc(sp_dve, 1)
                    dve.wait_ge(sp_dve, c + 4)
                    nc.vector.tensor_tensor(v, v, t, ALU.mult).then_inc(sp_dve, 1)
                    for i, (a, m) in enumerate(((ATANH[2], t), (ATANH[1], t), (ATANH[0], s))):
                        dve.wait_ge(sp_dve, c + 5 + i)
                        nc.vector.scalar_tensor_tensor(out=v, in0=v, scalar=a, in1=m, op0=ALU.add,
                                                       op1=ALU.mult).then_inc(sp_dve, 1)
                    dve.wait_ge(sp_dve, c + 8)
                    nc.vector.scalar_tensor_tensor(out=dt_sb[:, th, h, :], in0=xx, scalar=0.0, in1=v, op0=ALU.max,
                                                   op1=ALU.add).then_inc(sp_dve, 1)

            for h in range(HB):
                nc.vector.memset(decay_ps[h][:].rearrange("p (b l) -> p b l", b=BH)[:, :, 0:1],
                                 0.0).then_inc(decay_zeroed, 1)

            def scan(th, j):
                first = isinstance(j, int) and j == 0
                for h in range(HB):
                    dve.wait_ge(decay_ready, HB * j + h + 1)
                    dve.wait_ge(dbu_ready, HB * j + h + 1)
                    if not first:
                        dve.wait_ge(hc_ready, HB * j - HB + h + 1)
                    nc.vector.tensor_tensor_scan(hst[:, h, :], decay_ps[h][:], dbu[:, h, :], 0.0,
                                                 ALU.mult, ALU.add).then_inc(scanned, 1)
                dve.wait_ge(crep_made, j + 1)
                for h in range(HB):
                    dve.wait_ge(scanned, HB * j + h + 1)
                    if not first:
                        dve.wait_ge(summed, HB * j - HB + h + 1)
                    nc.vector.tensor_tensor(hc[:, h, :], hst[:, h, :], c_ps[:], ALU.mult).then_inc(hc_ready, 1)

            for th in range(TH):
                scan(th, th * NS)
                with dve.Fori(1, NS) as n:
                    scan(th, n + th * NS)
                dve.wait_ge(z_ready, NT)
                dve.wait_ge(summed, HB * NS * (th + 1))
                for h in range(HB):
                    nc.vector.tensor_tensor(yz[:, h, :], y_ps[h][:], zs_sb[:, th, h, :], ALU.mult).then_inc(yz_ready, 1)
                for i in range(BH):
                    dve.wait_ge(yz_T, BH * th + i + 1)
                    xv = x_sb[:, th * BH + i, :, :]
                    nc.vector.tensor_tensor(xv, yT_ps[i][:].rearrange("p (t d) -> p t d", t=LB), xv,
                                            ALU.add).then_inc(x1_ready, 1)
            dve.wait_ge(x1_ready, B)
            stats(1)
            for t in range(NT):
                nc.vector.tensor_scalar(xh[:, t, :], x_sb[:, t // LB, t % LB, :], mv[:, t, 0:1], rstd[:, t:t + 1],
                                        ALU.subtract, ALU.mult).then_inc(xh_ready, 1)
            dve.wait_ge(scored, 1)
            dve.wait_ge(in_small, 16 * 8)
            step = [0]
            rt = route

            def link(ins):
                step[0] += 1
                ins.then_inc(rt, 1)
                dve.wait_ge(rt, step[0])

            link(nc.vector.tensor_tensor(biased[:], score[:], bias_sb[:].unsqueeze(1).to_broadcast([P, NT, E]), ALU.add))
            for t in range(NT):
                i_ = nc.vector.max(top[:, t, :], biased[:, t, :])
                link(i_)
            for t in range(NT):
                i_ = nc.vector.max_index(topi[:, t, :], top[:, t, :], biased[:, t, :])
                link(i_)
            link(nc.vector.tensor_copy(topf[:], topi[:, :, 0:2]))
            en = expert_no[:].unsqueeze(1).to_broadcast([P, NT, E])
            link(nc.vector.tensor_tensor(m0[:], en, topf[:, :, 0:1].to_broadcast([P, NT, E]), ALU.is_equal))
            link(nc.vector.tensor_tensor(m1[:], en, topf[:, :, 1:2].to_broadcast([P, NT, E]), ALU.is_equal))
            link(nc.vector.tensor_tensor(m0[:], m0[:], m1[:], ALU.add))
            link(nc.vector.tensor_tensor(m0[:], m0[:], score[:], ALU.mult))
            link(nc.vector.tensor_reduce(wsum[:], m0[:], AX_X, ALU.add))
            link(nc.vector.tensor_scalar(wsum[:], wsum[:], 1e-20, None, ALU.add))
            link(nc.vector.reciprocal(winv[:], wsum[:]))
            link(nc.vector.memset(comb[:], 1.0))
            link(nc.vector.tensor_tensor(comb[:, :, 1:], m0[:], winv[:].unsqueeze(2).to_broadcast([P, NT, E]), ALU.mult))

            def gated(e, s0, t):
                s = s0 + t
                early = isinstance(s, int) and s < 2
                dve.wait_ge(silu_done, s + 1)
                if not early:
                    dve.wait_ge(h_T, s - 1)
                w = comb[:, t, e:e + 1] if isinstance(e, int) else comb[:, t, bass.ds(e, 1)]
                nc.vector.scalar_tensor_tensor(out=hm[:, t % 2, :], in0=bank[4 + t % 2][:, F:2 * F], scalar=w,
                                               in1=sg[:, t % 2, :], op0=ALU.mult, op1=ALU.mult).then_inc(hm_ready, 1)

            for t in range(NT):
                gated(0, 0, t)
            with dve.Fori(1, E + 1) as e:
                for t in range(NT):
                    gated(e, e * NT, t)
            dve.wait_ge(down_done, (E + 1) * NT)
            for t in range(NT):
                nc.vector.tensor_copy(o_sb[:, t, :], bank[t // 2][:, (t % 2) * H:(t % 2 + 1) * H]).then_inc(o_ready, 1)

        @block.tensor
        def _(pe):
            pe.wait_ge(consts, 1)
            pe.wait_ge(in_small, 16 * 8)
            for h in range(HB):
                nc.tensor.transpose(bank[4][:, h * (R + NBC):(h + 1) * (R + NBC)], xp_sb[:, h * P:(h + 1) * P],
                                    ident[0:R + NBC, 0:R + NBC])
            for h in range(HB):
                last = nc.tensor.transpose(bank[4][0:R, 128 + h * P:128 + (h + 1) * P], dp_sb[:, h, :], ident[:])
            last = nc.tensor.transpose(bank[4][:, 384:384 + 3 * HB], vec_rows[:], ident[0:3 * HB, 0:3 * HB])
            last.then_inc(small_T, 1)
            pe.wait_ge(in_ctx, 16)
            for th in range(TH):
                for i in range(BH * LB):
                    b, t = th * BH + i // LB, i % LB
                    last = nc.tensor.transpose(bank[th][:, i * P:(i + 1) * P], ctx_sb[:, b, t, :], ident[:])
                last.then_inc(ctx_T, 1)
            for h in range(HB):
                pe.wait_ge(wk_scaled, (h + 1) * K)
                for k in range(K):
                    last = nc.tensor.transpose(bank[2 + h][:, k * P:(k + 1) * P], wk[:, h, k, :], ident[:])
                last.then_inc(wk_T, 1)
            for g in range(TH * HB):
                th, h = divmod(g, HB)
                pe.wait_ge(wk_c, h + 1)
                pe.wait_ge(ctx_c, th + 1)
                for k in range(K):
                    last = nc.tensor.matmul(bank[(5 + g) % 8][:], wkT[:, h, k, :],
                                            ctxT[:, th * BH:(th + 1) * BH, k:k + L], start=(k == 0), stop=(k == K - 1))
                last.then_inc(conv_done, 1)
            pe.wait_ge(small_c, 3 * HB + 1)
            for th in range(TH):
                pe.wait_ge(u_ready, (th + 1) * HB)
                dl = bank[4] if th == 0 else bank[1]
                for h in range(HB):
                    last = nc.tensor.matmul(bank[2 + th][0:3 * NBC, :], bcT[:, h, :, :].rearrange("p a n -> p (a n)"),
                                            u_sb[:, th, h, :], start=(h == 0), stop=(h == HB - 1))
                last.then_inc(bc_done, 1)
                for h in range(HB):
                    last = nc.tensor.matmul(dl[0:R, :], dlT[:, h, :], u_sb[:, th, h, :], start=(h == 0), stop=(h == HB - 1))
                last.then_inc(dl_done, 1)
            for th in range(TH):
                pe.wait_ge(dl_c, th + 1)
                for h in range(HB):
                    nc.tensor.matmul(dtp_bank(th * HB + h), dpT[:, h, :], dl_sb[:, th, :],
                                     start=True, stop=True).then_inc(dtp_done, 1)

            pe.wait_ge(consts, 6)

            def spread(th, j, n):
                first = isinstance(j, int) and j == 0

                def sel(m):
                    return rowsel[:, m, :] if isinstance(m, int) else \
                        rowsel[:].rearrange("r n q -> r (n q)")[:, bass.ds(m * P, P)]
                if not first:
                    pe.wait_ge(brep_copied, j)
                nc.tensor.matmul(b_ps[:], sel(n), bc_hi[:, th, :], start=True, stop=True).then_inc(brep_made, 1)
                if not first:
                    pe.wait_ge(hc_ready, HB * j)
                nc.tensor.matmul(c_ps[:], sel(n + NS), bc_hi[:, th, :], start=True, stop=True).then_inc(crep_made, 1)

            def add_state(j, last_n):
                for h in range(HB):
                    pe.wait_ge(hc_ready, HB * j + h + 1)
                    nc.tensor.matmul(y_ps[h][:], ident[:], hc[:, h, :], start=False, stop=last_n,
                                     skip_group_check=True).then_inc(summed, 1)

            for th in range(TH):
                pe.wait_ge(du_ready, HB * (th + 1))
                if th == 0:
                    pe.wait_ge(split_dve, 5 * TH)
                    pe.wait_ge(spx, TH * HB)
                    pe.wait_ge(dl_c, TH)
                if th >= 1:
                    pe.wait_ge(yz_ready, HB * th)
                spread(th, th * NS, 0)
                for h in range(HB):
                    nc.tensor.matmul(y_ps[h][:], ident[:], du_sb[:, th, h, :], start=True, stop=False,
                                     skip_group_check=True)
                with pe.Fori(1, NS) as n:
                    spread(th, n + th * NS, n)
                    add_state(n + (th * NS - 1), False)
                add_state((th + 1) * NS - 1, True)
                pe.wait_ge(yz_ready, HB * (th + 1))
                if th >= 1:
                    pe.wait_ge(x1_ready, BH * th)
                for i in range(BH):
                    for t in range(LB):
                        for h in range(HB):
                            last = nc.tensor.transpose(yT_ps[i][:, t * H + h * P:t * H + (h + 1) * P],
                                                       yz[:, h, i * L + t * P:i * L + (t + 1) * P], ident[:])
                    last.then_inc(yz_T, 1)
            for k in range(HB):
                for t in range(NT):
                    pe.wait_ge(xh_ready, t + 1)
                    col = (k * NT + t) * P
                    last = nc.tensor.transpose(bank[col // 512][:, col % 512:col % 512 + P],
                                               xh[:, t, k * P:(k + 1) * P], ident[:])
                    if t % 4 == 3:
                        last.then_inc(xh_T, 1)
            pe.wait_ge(xh_c, 4)
            for t in range(NT):
                for k in range(HB):
                    last = nc.tensor.matmul(bank[4][:, t * E:(t + 1) * E], xhT[:, k, t, :], gatew_sb[:, k, :],
                                            start=(k == 0), stop=(k == HB - 1))
            last.then_inc(logits, 1)
            for t in range(NT):
                nc.tensor.matmul(bank[t // 2][:, (t % 2) * H:(t % 2 + 1) * H], ident[:], x_sb[:, t // LB, t % LB, :],
                                 start=(t % 2 == 0), stop=False, skip_group_check=True)
            pe.wait_ge(in_ffn, 16 * 6)
            pe.wait_ge(scored, 1)

            def gate_up(e, s0, t):
                s = s0 + t
                if not (isinstance(s, int) and s < 2):
                    pe.wait_ge(hm_ready, s - 1)
                for k in range(HB):
                    w = gu_sb[:, e, k, :] if isinstance(e, int) else \
                        gu_sb[:].rearrange("p e k f -> p (e k f)")[:, bass.ds(e * (HB * 2 * F) + k * 2 * F, 2 * F)]
                    last = nc.tensor.matmul(bank[4 + t % 2][:, 0:2 * F], xhT[:, k, t, :], w,
                                            start=(k == 0), stop=(k == HB - 1))
                last.then_inc(gu_made, 1)

            def turn(s0, t):
                s = s0 + t
                pe.wait_ge(hm_ready, s + 1)
                if not (isinstance(s, int) and s < 2):
                    pe.wait_ge(hT_ready, s - 1)
                nc.tensor.transpose(bank[6 + t % 2][:, 0:P], hm[:, t % 2, :], ident[:]).then_inc(h_T, 1)

            def down(e, s0, t):
                s = s0 + t
                pe.wait_ge(hT_ready, s + 1)
                w = dn_sb[:, e, :] if isinstance(e, int) else \
                    dn_sb[:].rearrange("p e f -> p (e f)")[:, bass.ds(e * H, H)]
                tt = t % NT
                nc.tensor.matmul(bank[tt // 2][:, (tt % 2) * H:(tt % 2 + 1) * H], hT[:, t % 2, :], w,
                                 start=False, stop=True, skip_group_check=True).then_inc(down_done, 1)

            for t in range(NT):
                gate_up(0, 0, t)
                if t >= 1:
                    turn(0, t - 1)
                if t >= 2:
                    down(0, 0, t - 2)
            with pe.Fori(1, E + 1) as e:
                for t in range(NT):
                    gate_up(e, e * NT, t)
                    turn(e * NT, t - 1)
                    down(e if t >= 2 else e - 1, e * NT, t - 2)
            turn((E + 1) * NT, -1)
            down(E, (E + 1) * NT, -2)
            down(E, (E + 1) * NT, -1)


_INS = ['x', 'ctx_1024', 'L0_xattn_in_proj_w', 'L0_xattn_conv_w', 'L0_xattn_conv_b', 'L0_xattn_x_proj_w',
        'L0_xattn_dt_proj_w', 'L0_xattn_dt_proj_b', 'L0_xattn_A_log', 'L0_xattn_D', 'L0_ffn_gate_w',
        'L0_ffn_expert_bias', 'L0_ffn_shared_gate_w', 'L0_ffn_shared_up_w', 'L0_ffn_shared_down_w',
        'L0_ffn_experts_gate_up', 'L0_ffn_experts_down']
_OUTS = [((4, 256, 256), 'float32')]


def kernel(**inputs):
    import numpy as _np
    import concourse.bacc as _bacc
    from concourse import mybir as _mybir
    from concourse.bass_utils import run_bass_kernel_spmd as _run

    nc = _bacc.Bacc("TRN2", target_bir_lowering=False, num_devices=1)
    arrays, args = {}, []
    for name in _INS:
        a = _np.ascontiguousarray(inputs[name])
        arrays[f"in_{name}_dram"] = a
        args.append(nc.dram_tensor(f"in_{name}_dram", a.shape, _mybir.dt.from_np(a.dtype), kind="ExternalInput").ap())
    for i, (shape, dtype) in enumerate(_OUTS):
        dt = _mybir.dt.from_np(_np.dtype(dtype))
        args.append(nc.dram_tensor(f"out_{i}_dram", shape, dt, kind="ExternalOutput").ap())
    block_kernel(nc, *args)
    r = _run(nc, [arrays], core_ids=[0])
    got = tuple(r.results[0][f"out_{i}_dram"] for i in range(len(_OUTS)))
    return got[0]
```

```python
from contextlib import ExitStack

import concourse.bass as bass
from concourse import mybir
import numpy as np

ALU = mybir.AluOpType
ACT = mybir.ActivationFunctionType
F32 = mybir.dt.float32
BF16 = mybir.dt.bfloat16
U32 = mybir.dt.uint32
AX_X = mybir.AxisListType.X

P = 128
LN2 = 0.6931471805599453
ATANH = (2.0000000012778267, 0.6666639578183403, 0.4002308285536912, 0.27970779753899433, 0.2818452560443701)


def block_kernel(nc, x, ctxT_in, inwT_in, taps_in, small_in, gu_in, dn_in, out):
    B, L, H = x.shape
    DM = ctxT_in.shape[0]
    K = taps_in.shape[1]
    E = gu_in.shape[1] - 1
    F = dn_in.shape[0]
    DI, NS, R = 256, 16, 8
    HB = DI // P
    LB = L // P
    NT = B * LB
    BH = 2
    TH = B // BH
    C = BH * L
    NBC = 2 * NS
    NPROJ = 3 * NBC + R
    SMALL = small_in.shape[1]
    assert C == 512 and DM == P and F == P and HB == 2 and LB == 2 and H == HB * P and NBC == 32
    EPS = 1e-5

    with ExitStack() as stack:
        def sb(name, shape, dt=F32):
            return stack.enter_context(nc.sbuf_tensor(name, shape, dt))

        def sem(name):
            return stack.enter_context(nc.semaphore(name))

        bank = [stack.enter_context(nc.psum_tensor(f"bank{i}", [P, 512], F32)) for i in range(8)]

        ctxT = sb("ctxT", [P, B, K - 1 + L])
        inwT = sb("inwT", [P, HB, P])
        cw_rep = sb("cw_rep", [P, HB, K, P])
        small = sb("small", [P, SMALL])
        x_sb = sb("x_sb", [P, B, LB, H])
        gu_sb = sb("gu_sb", [P, E + 1, HB, 2 * F])
        dn_sb = sb("dn_sb", [P, E + 1, H])

        def view(at, *dims):
            n = int(np.prod(dims))
            v = small[:, at:at + n]
            return v if len(dims) == 1 else v.rearrange(f"p (a b) -> p a b", a=dims[0])
        projT = view(0, HB, NPROJ)
        cb_sb, db_sb, d_sb = (view(HB * NPROJ + i * HB, HB) for i in range(3))
        al_sb = view(HB * NPROJ + 3 * HB, HB, NS)
        gatew_sb = view(HB * NPROJ + 3 * HB + HB * NS, HB, E)
        bias_sb = view(HB * NPROJ + 3 * HB + HB * NS + HB * E, E)
        dpT = small[3 * NBC:NPROJ, SMALL - DI:SMALL].rearrange("r (h q) -> r h q", h=HB)

        ident = sb("ident", [P, P])
        rowsel = sb("rowsel", [3 * NBC, NBC, P], BF16)
        rowsel1 = sb("rowsel1", [3 * NBC, NBC])
        minus_half = sb("minus_half", [P, NT])
        expert_no = sb("expert_no", [P, E])

        wkT = sb("wkT", [P, HB, K, P])
        A_sb = sb("A_sb", [P, HB, NS])
        u_sb = sb("u_sb", [P, TH, HB, C])
        du_sb = sb("du_sb", [P, TH, HB, C])
        dt_sb = sb("dt_sb", [P, TH, HB, C])
        dtu_sb = sb("dtu_sb", [P, TH, HB, C])
        zs_sb = sb("zs_sb", [P, TH, HB, C])
        bc3 = sb("bc3", [3 * NBC, TH, C], BF16)
        bc_res = sb("bc_res", [3 * NBC, TH, C])
        dl_sb = sb("dl_sb", [P, TH, C])
        soft = {n: sb(f"soft_{n}", [P, TH, HB, C]) for n in ("abs", "relu", "s", "t", "v")}
        st6 = sb("st6", [P, NT, 6])
        mv = sb("mv", [P, NT, 2])
        ve = sb("ve", [P, NT])
        rstd = sb("rstd", [P, NT])
        nmr = sb("nmr", [P, NT])
        brep = sb("brep", [P, 2, C])
        dbu = sb("dbu", [P, 2, HB, C])
        hst = sb("hst", [P, HB, C])
        hc = sb("hc", [P, 2, HB, C])
        yz = du_sb

        xh = soft["abs"][:].rearrange("p a h c -> p (a h c)").rearrange("p (t d) -> p t d", t=NT)
        xhT = soft["s"][:].rearrange("p a h c -> p (a h c)").rearrange("p (k t q) -> p k t q", k=HB, t=NT)
        o_sb = soft["t"][:].rearrange("p a h c -> p (a h c)").rearrange("p (t d) -> p t d", t=NT)
        score = sb("score", [P, NT, E])
        biased = sb("biased", [P, NT, E])
        top = sb("top", [P, NT, 8])
        topi = sb("topi", [P, NT, 8], U32)
        topf = sb("topf", [P, NT, 2])
        m0 = sb("m0", [P, NT, E])
        m1 = sb("m1", [P, NT, E])
        wsum = sb("wsum", [P, NT])
        winv = sb("winv", [P, NT])
        comb = sb("comb", [P, NT, E + 1])
        sg = sb("sg", [P, 2, F])
        hm = sb("hm", [P, 2, F])
        hT = sb("hT", [P, 2, P])

        in_first = sem("in_first")
        in_small = sem("in_small")
        in_taps = sem("in_taps")
        in_x = sem("in_x")
        in_ffn = sem("in_ffn")
        out_done = sem("out_done")
        ident_zeroed = sem("ident_zeroed")
        ident_ready = sem("ident_ready")
        consts = sem("consts")
        rowsel1_ready = sem("rowsel1_ready")
        rowsel_ready = sem("rowsel_ready")
        taps_ready = sem("taps_ready")
        conv_done = sem("conv_done")
        u_ready = sem("u_ready")
        proj_done = sem("proj_done")
        dl_copied = sem("dl_copied")
        split = sem("split")
        dtp_done = sem("dtp_done")
        soft_act = sem("soft_act")
        soft_dve = sem("soft_dve")
        du_ready = sem("du_ready")
        dtu_ready = sem("dtu_ready")
        bn = sem("bn")
        var_ready = sem("var_ready")
        rstd_ready = sem("rstd_ready")
        nmr_ready = sem("nmr_ready")
        z_ready = sem("z_ready")
        a_exp = sem("a_exp")
        a_ready = sem("a_ready")
        decay_zeroed = sem("decay_zeroed")
        brep_made = sem("brep_made")
        brep_copied = sem("brep_copied")
        crep_made = sem("crep_made")
        decay_ready = sem("decay_ready")
        dbu_ready = sem("dbu_ready")
        scanned = sem("scanned")
        hc_ready = sem("hc_ready")
        summed = sem("summed")
        yz_ready = sem("yz_ready")
        yz_T = sem("yz_T")
        x1_ready = sem("x1_ready")
        xh_ready = sem("xh_ready")
        xh_T = sem("xh_T")
        xh_c = sem("xh_c")
        logits = sem("logits")
        scored = sem("scored")
        route = sem("route")
        gu_made = sem("gu_made")
        silu_done = sem("silu_done")
        hm_ready = sem("hm_ready")
        h_T = sem("h_T")
        hT_ready = sem("hT_ready")
        down_done = sem("down_done")
        o_ready = sem("o_ready")

        conv_ps = [bank[4], bank[5], bank[6], bank[7]]
        proj_ps = [bank[0], bank[1]]
        dtp_ps = [bank[2], bank[3], bank[4], bank[5]]
        y_ps = [bank[0], bank[1]]
        b_ps, c_ps = bank[2], bank[3]
        decay_ps = [[bank[4], bank[5]], [bank[6], bank[7]]]
        yT_ps = [bank[0], bank[1], bank[2], bank[3]]

        def act_stage(th, i, h):
            return HB * (6 * th + i) + h + 1

        def dve_stage(th, i, h):
            return HB * (7 * th + i) + h + 1

        block = stack.enter_context(nc.Block())

        @block.sync
        def _(sp):
            sp.dma_start(ctxT[:], ctxT_in).then_inc(in_first, 16)
            sp.dma_start(cw_rep[:], taps_in.partition_broadcast(P)).then_inc(in_taps, 16)
            sp.dma_start(x_sb[:], x.rearrange("b (t p) d -> p b t d", p=P)).then_inc(in_x, 16)
            sp.dma_start(gu_sb[:], gu_in).then_inc(in_ffn, 16)
            sp.dma_start(dn_sb[:], dn_in).then_inc(in_ffn, 16)
            for t in range(NT):
                sp.wait_ge(o_ready, t + 1)
                sp.dma_start(out[t // LB, (t % LB) * P:(t % LB + 1) * P, :], o_sb[:, t, :]).then_inc(out_done, 16)
            sp.wait_ge(out_done, 16 * NT)

        @block.gpsimd
        def _(pool):
            nc.gpsimd.memset(ident[:], 0.0).then_inc(ident_zeroed, 1)
            nc.gpsimd.memset(minus_half[:], -0.5).then_inc(consts, 1)
            pool.wait_ge(ident_zeroed, 1)
            nc.gpsimd.affine_select(out=ident[:], in_=ident[:], compare_op=ALU.not_equal, fill=1.0, base=0,
                                    pattern=[[-1, P]], channel_multiplier=1).then_inc(ident_ready, 1)
            nc.gpsimd.iota(expert_no[:], [[1, E]], base=0, channel_multiplier=0,
                           allow_small_or_imprecise_dtypes=True).then_inc(consts, 1)
            pool.wait_ge(consts, 1)
            pool.wait_ge(var_ready, 1)
            nc.gpsimd.tensor_tensor(rstd[:], ve[:], minus_half[:], ALU.pow).then_inc(rstd_ready, 1)
            pool.wait_ge(in_small, 16)
            for k in range(TH * HB):
                th, h = divmod(k, HB)
                pool.wait_ge(u_ready, k + 1)
                nc.gpsimd.tensor_scalar(du_sb[:, th, h, :], u_sb[:, th, h, :], d_sb[:, h:h + 1], 1.0,
                                        ALU.mult, ALU.mult).then_inc(du_ready, 1)

            def step_input(th):
                for h in range(HB):
                    pool.wait_ge(soft_dve, dve_stage(th, 6, h))
                    nc.gpsimd.tensor_tensor(dtu_sb[:, th, h, :], dt_sb[:, th, h, :], u_sb[:, th, h, :],
                                            ALU.mult).then_inc(dtu_ready, 1)

            def drive(th, j, q):
                pool.wait_ge(brep_copied, j + 1)
                for h in range(HB):
                    if not (isinstance(j, int) and j < 2):
                        pool.wait_ge(scanned, HB * j - 2 * HB + h + 1)
                    nc.gpsimd.tensor_tensor(dbu[:, q, h, :], dtu_sb[:, th, h, :], brep[:, q, :],
                                            ALU.mult).then_inc(dbu_ready, 1)

            for th in range(TH):
                step_input(th)
                pool.wait_ge(dtu_ready, (th + 1) * HB)
                for q in range(2):
                    drive(th, th * NS + q, q)
                with pool.Fori(1, NS // 2) as m:
                    for q in range(2):
                        drive(th, m * 2 + (th * NS + q), q)
            pool.wait_ge(var_ready, 2)
            nc.gpsimd.tensor_tensor(rstd[:], ve[:], minus_half[:], ALU.pow).then_inc(rstd_ready, 1)

        @block.scalar
        def _(act):
            act.dma_start(inwT[:], inwT_in).then_inc(in_first, 16)
            act.dma_start(small[:], small_in).then_inc(in_small, 16)

            def make_u(k):
                th, h = divmod(k, HB)
                act.wait_ge(conv_done, k + 1)
                nc.scalar.activation(u_sb[:, th, h, :], conv_ps[k][:], ACT.Silu,
                                     bias=cb_sb[:, h:h + 1]).then_inc(u_ready, 1)

            def make_z(b):
                for h in range(HB):
                    t = b * HB + h
                    nc.scalar.activation(zs_sb[:, b // BH, h, (b % BH) * L:(b % BH + 1) * L], x_sb[:, b, h, :],
                                         ACT.Silu, bias=nmr[:, t:t + 1], scale=rstd[:, t:t + 1]).then_inc(z_ready, 1)
            act.wait_ge(in_small, 16)
            make_u(0)
            make_u(1)
            act.wait_ge(nmr_ready, 1)
            make_z(0)
            make_z(1)
            make_u(2)
            make_z(2)
            make_z(3)
            make_u(3)
            nc.scalar.activation(A_sb[:], al_sb, ACT.Exp).then_inc(a_exp, 1)

            for th in range(TH):
                w = {n: [v[:, th, h, :] for h in range(HB)] for n, v in soft.items()}
                for h in range(HB):
                    act.wait_ge(dtp_done, th * HB + h + 1)
                    nc.scalar.activation(w["abs"][h], dtp_ps[th * HB + h][:], ACT.Abs,
                                         bias=db_sb[:, h:h + 1]).then_inc(soft_act, 1)
                for h in range(HB):
                    nc.scalar.activation(w["relu"][h], dtp_ps[th * HB + h][:], ACT.Relu,
                                         bias=db_sb[:, h:h + 1]).then_inc(soft_act, 1)
                for h in range(HB):
                    act.wait_ge(soft_act, act_stage(th, 0, h))
                    nc.scalar.activation(w["s"][h], w["abs"][h], ACT.Exp, scale=-1.0).then_inc(soft_act, 1)
                for h in range(HB):
                    act.wait_ge(soft_act, act_stage(th, 2, h))
                    nc.scalar.activation(w["t"][h], w["s"][h], ACT.Ln, bias=1.0, scale=0.5).then_inc(soft_act, 1)
                for h in range(HB):
                    act.wait_ge(soft_dve, dve_stage(th, 0, h))
                    nc.scalar.activation(w["s"][h], w["v"][h], ACT.Exp, scale=-1.0).then_inc(soft_act, 1)
                for h in range(HB):
                    act.wait_ge(soft_act, act_stage(th, 4, h))
                    nc.scalar.activation(w["t"][h], w["s"][h], ACT.Square).then_inc(soft_act, 1)

            def decay(th, n, j, q):
                first = isinstance(j, int) and j < 2
                act.wait_ge(brep_made, j + 1)
                if not first:
                    act.wait_ge(dbu_ready, HB * j - HB)
                nc.scalar.copy(brep[:, q, :], b_ps[:]).then_inc(brep_copied, 1)
                for h in range(HB):
                    if not first:
                        act.wait_ge(scanned, HB * j - 2 * HB + h + 1)
                    v = decay_ps[q][h][:].rearrange("p (b l) -> p b l", b=BH)[:, :, 1:]
                    d = dt_sb[:, th, h, :].rearrange("p (b l) -> p b l", b=BH)[:, :, 1:]
                    nc.scalar.activation(v, d, ACT.Exp, scale=A_sb[:, h, bass.ds(n, 1)]).then_inc(decay_ready, 1)

            act.wait_ge(a_ready, 1)
            act.wait_ge(decay_zeroed, 2 * HB)
            for th in range(TH):
                act.wait_ge(soft_dve, dve_stage(th, 6, HB - 1))
                for q in range(2):
                    decay(th, q, th * NS + q, q)
                with act.Fori(1, NS // 2) as m:
                    for q in range(2):
                        decay(th, m * 2 + q, m * 2 + (th * NS + q), q)

            for i in range(4):
                act.wait_ge(xh_T, i + 1)
                nc.scalar.copy(xhT.rearrange("p k t q -> p (k t q)")[:, i * 512:(i + 1) * 512], bank[i][:]).then_inc(xh_c, 1)
            act.wait_ge(logits, 1)
            nc.scalar.activation(score[:].rearrange("p t e -> p (t e)"), bank[4][:, 0:NT * E], ACT.Sigmoid).then_inc(scored, 1)

            def gate(s0, t):
                s = s0 + t
                early = isinstance(s, int) and s < 2
                act.wait_ge(gu_made, s + 1)
                if not early:
                    act.wait_ge(hm_ready, s - 1)
                nc.scalar.activation(sg[:, t % 2, :], bank[4 + t % 2][:, 0:F], ACT.Silu).then_inc(silu_done, 1)

            def move_hT(s0, t):
                s = s0 + t
                early = isinstance(s, int) and s < 2
                act.wait_ge(h_T, s + 1)
                if not early:
                    act.wait_ge(down_done, s - 1)
                nc.scalar.copy(hT[:, t % 2, :], bank[6 + t % 2][:, 0:P]).then_inc(hT_ready, 1)

            for t in range(NT):
                gate(0, t)
                if t >= 1:
                    move_hT(0, t - 1)
            with act.Fori(1, E + 1) as e:
                for t in range(NT):
                    gate(e * NT, t)
                    move_hT(e * NT, t - 1)
            move_hT((E + 1) * NT, -1)

        @block.vector
        def _(dve):
            dve.wait_ge(in_first, 32)
            dve.wait_ge(in_taps, 16)
            for h in range(HB):
                nc.vector.tensor_tensor(wkT[:, h, :, :], inwT[:, h, :].unsqueeze(1).to_broadcast([P, K, P]),
                                        cw_rep[:, h, :, :], ALU.mult).then_inc(taps_ready, 1)

            def stats(phase):
                for t in range(NT):
                    nc.vector.bn_stats(st6[:, t, :], x_sb[:, t // LB, t % LB, :]).then_inc(bn, 1)
                for t in range(NT):
                    dve.wait_ge(bn, phase * 2 * NT + t + 1)
                    nc.vector.bn_aggr(mv[:, t, :], st6[:, t, :]).then_inc(bn, 1)
                dve.wait_ge(bn, phase * 2 * NT + 2 * NT)
                nc.vector.tensor_scalar(ve[:], mv[:, :, 1], EPS, None, ALU.add).then_inc(var_ready, 1)

            dve.wait_ge(in_x, 16)
            stats(0)
            dve.wait_ge(ident_ready, 1)
            idn = [ident[0:3 * NBC, q * NBC:(q + 1) * NBC] for q in range(3)]
            nc.vector.tensor_tensor(rowsel1[:], idn[0], idn[1], ALU.add).then_inc(rowsel1_ready, 1)
            dve.wait_ge(rowsel1_ready, 1)
            nc.vector.tensor_tensor(rowsel1[:], rowsel1[:], idn[2], ALU.add).then_inc(rowsel1_ready, 1)
            dve.wait_ge(rstd_ready, 1)
            nc.vector.scalar_tensor_tensor(out=nmr[:], in0=mv[:, :, 0], scalar=-1.0, in1=rstd[:],
                                           op0=ALU.mult, op1=ALU.mult).then_inc(nmr_ready, 1)
            dve.wait_ge(rowsel1_ready, 2)
            nc.vector.tensor_copy(rowsel[:], rowsel1[:].unsqueeze(2).to_broadcast([3 * NBC, NBC, P])).then_inc(rowsel_ready, 1)

            def project(th):
                dve.wait_ge(proj_done, th + 1)
                nc.vector.tensor_copy(dl_sb[3 * NBC:NPROJ, th, :], proj_ps[th][3 * NBC:NPROJ, :]).then_inc(dl_copied, 1)
                X = proj_ps[th][0:3 * NBC, :]
                c = 5 * th
                nc.vector.tensor_copy(bc3[:, th, :], X).then_inc(split, 1)
                dve.wait_ge(split, c + 1)
                nc.vector.tensor_tensor(bc_res[:, th, :], X, bc3[:, th, :], ALU.subtract).then_inc(split, 1)
                dve.wait_ge(split, c + 2)
                for q in (1, 2):
                    rows = slice(q * NBC, (q + 1) * NBC)
                    nc.vector.tensor_copy(bc3[rows, th, :], bc_res[rows, th, :]).then_inc(split, 1)
                dve.wait_ge(split, c + 4)
                nc.vector.tensor_tensor(bc3[rows, th, :], bc_res[rows, th, :], bc3[rows, th, :],
                                        ALU.subtract).then_inc(split, 1)

            def softplus(th):
                w = {n: [v[:, th, h, :] for h in range(HB)] for n, v in soft.items()}
                for h in range(HB):
                    dve.wait_ge(soft_act, act_stage(th, 3, h))
                    nc.vector.scalar_tensor_tensor(out=w["v"][h], in0=w["abs"][h], scalar=LN2, in1=w["t"][h],
                                                   op0=ALU.add, op1=ALU.add).then_inc(soft_dve, 1)
                for h in range(HB):
                    dve.wait_ge(soft_act, act_stage(th, 5, h))
                    nc.vector.tensor_scalar(w["v"][h], w["t"][h], ATANH[4], ATANH[3], ALU.mult, ALU.add).then_inc(soft_dve, 1)
                for h in range(HB):
                    dve.wait_ge(soft_dve, dve_stage(th, 1, h))
                    nc.vector.tensor_tensor(w["v"][h], w["v"][h], w["t"][h], ALU.mult).then_inc(soft_dve, 1)
                for i, (c, m) in enumerate(((ATANH[2], "t"), (ATANH[1], "t"), (ATANH[0], "s"))):
                    for h in range(HB):
                        dve.wait_ge(soft_dve, dve_stage(th, 2 + i, h))
                        nc.vector.scalar_tensor_tensor(out=w["v"][h], in0=w["v"][h], scalar=c, in1=w[m][h],
                                                       op0=ALU.add, op1=ALU.mult).then_inc(soft_dve, 1)
                for h in range(HB):
                    dve.wait_ge(soft_dve, dve_stage(th, 5, h))
                    nc.vector.tensor_tensor(dt_sb[:, th, h, :], w["v"][h], w["relu"][h], ALU.add).then_inc(soft_dve, 1)

            project(0)
            project(1)
            dve.wait_ge(a_exp, 1)
            nc.vector.tensor_scalar(A_sb[:], A_sb[:], -1.0, None, ALU.mult).then_inc(a_ready, 1)
            softplus(0)
            dve.wait_ge(u_ready, TH * HB)
            dve.wait_ge(soft_act, act_stage(1, 1, HB - 1))
            for q in range(2):
                for h in range(HB):
                    nc.vector.memset(decay_ps[q][h][:].rearrange("p (b l) -> p b l", b=BH)[:, :, 0:1],
                                     0.0).then_inc(decay_zeroed, 1)
            softplus(1)

            def scan(j, q):
                first = isinstance(j, int) and j < 2
                for h in range(HB):
                    dve.wait_ge(decay_ready, HB * j + h + 1)
                    dve.wait_ge(dbu_ready, HB * j + h + 1)
                    if not (isinstance(j, int) and j == 0):
                        dve.wait_ge(hc_ready, HB * j - HB + h + 1)
                    nc.vector.tensor_tensor_scan(hst[:, h, :], decay_ps[q][h][:], dbu[:, q, h, :], 0.0,
                                                 ALU.mult, ALU.add).then_inc(scanned, 1)
                dve.wait_ge(crep_made, j + 1)
                for h in range(HB):
                    dve.wait_ge(scanned, HB * j + h + 1)
                    if not first:
                        dve.wait_ge(summed, HB * j - 2 * HB + h + 1)
                    nc.vector.tensor_tensor(hc[:, q, h, :], hst[:, h, :], c_ps[:], ALU.mult).then_inc(hc_ready, 1)

            def gate_y(th):
                dve.wait_ge(z_ready, NT)
                dve.wait_ge(summed, HB * NS * (th + 1))
                for h in range(HB):
                    nc.vector.tensor_tensor(yz[:, th, h, :], y_ps[h][:], zs_sb[:, th, h, :], ALU.mult).then_inc(yz_ready, 1)

            for th in range(TH):
                scan(th * NS, 0)
                if th >= 1:
                    gate_y(th - 1)
                scan(th * NS + 1, 1)
                with dve.Fori(1, NS // 2) as m:
                    for q in range(2):
                        scan(m * 2 + (th * NS + q), q)
            gate_y(TH - 1)
            for b in range(B):
                dve.wait_ge(yz_T, b + 1)
                xv = x_sb[:, b, :, :]
                nc.vector.tensor_tensor(xv, yT_ps[b][:].rearrange("p (t d) -> p t d", t=LB), xv, ALU.add).then_inc(x1_ready, 1)
            dve.wait_ge(x1_ready, B)
            stats(1)
            dve.wait_ge(rstd_ready, 2)
            for t in range(NT):
                nc.vector.tensor_scalar(xh[:, t, :], x_sb[:, t // LB, t % LB, :], mv[:, t, 0:1], rstd[:, t:t + 1],
                                        ALU.subtract, ALU.mult).then_inc(xh_ready, 1)
            dve.wait_ge(scored, 1)
            step = [0]
            rt = route

            def link(ins):
                step[0] += 1
                ins.then_inc(rt, 1)
                dve.wait_ge(rt, step[0])

            link(nc.vector.tensor_tensor(biased[:], score[:], bias_sb.unsqueeze(1).to_broadcast([P, NT, E]), ALU.add))
            for t in range(NT):
                i_ = nc.vector.max(top[:, t, :], biased[:, t, :])
                link(i_)
            for t in range(NT):
                i_ = nc.vector.max_index(topi[:, t, :], top[:, t, :], biased[:, t, :])
                link(i_)
            link(nc.vector.tensor_copy(topf[:], topi[:, :, 0:2]))
            en = expert_no[:].unsqueeze(1).to_broadcast([P, NT, E])
            link(nc.vector.tensor_tensor(m0[:], en, topf[:, :, 0:1].to_broadcast([P, NT, E]), ALU.is_equal))
            link(nc.vector.tensor_tensor(m1[:], en, topf[:, :, 1:2].to_broadcast([P, NT, E]), ALU.is_equal))
            link(nc.vector.tensor_tensor(m0[:], m0[:], m1[:], ALU.add))
            link(nc.vector.tensor_tensor(m0[:], m0[:], score[:], ALU.mult))
            link(nc.vector.tensor_reduce(wsum[:], m0[:], AX_X, ALU.add))
            link(nc.vector.tensor_scalar(wsum[:], wsum[:], 1e-20, None, ALU.add))
            link(nc.vector.reciprocal(winv[:], wsum[:]))
            link(nc.vector.memset(comb[:], 1.0))
            link(nc.vector.tensor_tensor(comb[:, :, 1:], m0[:], winv[:].unsqueeze(2).to_broadcast([P, NT, E]), ALU.mult))

            def gated(e, s0, t):
                s = s0 + t
                early = isinstance(s, int) and s < 2
                dve.wait_ge(silu_done, s + 1)
                if not early:
                    dve.wait_ge(h_T, s - 1)
                w = comb[:, t, e:e + 1] if isinstance(e, int) else comb[:, t, bass.ds(e, 1)]
                nc.vector.scalar_tensor_tensor(out=hm[:, t % 2, :], in0=bank[4 + t % 2][:, F:2 * F], scalar=w,
                                               in1=sg[:, t % 2, :], op0=ALU.mult, op1=ALU.mult).then_inc(hm_ready, 1)

            for t in range(NT):
                gated(0, 0, t)
            with dve.Fori(1, E + 1) as e:
                for t in range(NT):
                    gated(e, e * NT, t)
            dve.wait_ge(down_done, (E + 1) * NT)
            for t in range(NT):
                nc.vector.tensor_copy(o_sb[:, t, :], bank[t // 2][:, (t % 2) * H:(t % 2 + 1) * H]).then_inc(o_ready, 1)

        @block.tensor
        def _(pe):
            def conv(k):
                th, h = divmod(k, HB)
                pe.wait_ge(taps_ready, h + 1)
                for i in range(K):
                    last = nc.tensor.matmul(conv_ps[k][:], wkT[:, h, i, :], ctxT[:, th * BH:(th + 1) * BH, i:i + L],
                                            start=(i == 0), stop=(i == K - 1))
                last.then_inc(conv_done, 1)

            def proj(th):
                pe.wait_ge(u_ready, (th + 1) * HB)
                for h in range(HB):
                    last = nc.tensor.matmul(proj_ps[th][0:NPROJ, :], projT[:, h, :], u_sb[:, th, h, :],
                                            start=(h == 0), stop=(h == HB - 1))
                last.then_inc(proj_done, 1)

            def steps(th):
                pe.wait_ge(dl_copied, th + 1)
                for h in range(HB):
                    nc.tensor.matmul(dtp_ps[th * HB + h][:], dpT[:, h, :], dl_sb[3 * NBC:NPROJ, th, :],
                                     start=True, stop=True).then_inc(dtp_done, 1)

            pe.wait_ge(in_first, 32)
            conv(0)
            conv(1)
            pe.wait_ge(in_small, 16)
            proj(0)
            conv(2)
            steps(0)
            conv(3)
            proj(1)
            steps(1)

            def spread_b(th, n, j):
                if not (isinstance(j, int) and j == 0):
                    pe.wait_ge(brep_copied, j)
                nc.tensor.matmul(b_ps[:], sel(n), bc3[:, th, :], start=True, stop=True).then_inc(brep_made, 1)

            def spread_c(th, n, j):
                if not (isinstance(j, int) and j == 0):
                    pe.wait_ge(hc_ready, HB * j)
                nc.tensor.matmul(c_ps[:], sel(n + NS), bc3[:, th, :], start=True, stop=True).then_inc(crep_made, 1)

            def sel(m):
                return rowsel[:, m, :] if isinstance(m, int) else \
                    rowsel[:].rearrange("r n q -> r (n q)")[:, bass.ds(m * P, P)]

            def add_state(j, q):
                for h in range(HB):
                    nc.tensor.matmul(y_ps[h][:], ident[:], hc[:, q, h, :], start=False, stop=False,
                                     skip_group_check=True).then_inc(summed, 1)

            def open_y(th):
                pe.wait_ge(du_ready, HB * (th + 1))
                if th >= 1:
                    pe.wait_ge(yz_ready, HB * th)
                for h in range(HB):
                    nc.tensor.matmul(y_ps[h][:], ident[:], du_sb[:, th, h, :], start=True, stop=False,
                                     skip_group_check=True)

            pe.wait_ge(rowsel_ready, 1)
            pe.wait_ge(split, 5 * TH)
            pe.wait_ge(soft_act, act_stage(0, 1, HB - 1))
            spread_b(0, 0, 0)
            for th in range(TH):
                j0 = th * NS
                spread_b(th, 1, j0 + 1)
                spread_c(th, 0, j0)
                if th >= 1:
                    add_state(j0 - 1, 1)
                open_y(th)
                with pe.Fori(1, NS // 2) as m:
                    for q in range(2):
                        n = m * 2 + (q - 1)
                        spread_b(th, n + 1, n + (j0 + 1))
                        spread_c(th, n, n + j0)
                        add_state(n + (j0 - 1), q)
                if th + 1 < TH:
                    spread_b(th + 1, 0, j0 + NS)
                spread_c(th, NS - 1, j0 + NS - 1)
                add_state(j0 + NS - 2, 0)
            pe.wait_ge(hc_ready, TH * NS * HB)
            add_state(TH * NS - 1, 1)
            pe.wait_ge(yz_ready, HB * TH)
            for b in range(B):
                th, i = divmod(b, BH)
                for t in range(LB):
                    for h in range(HB):
                        last = nc.tensor.transpose(yT_ps[b][:, t * H + h * P:t * H + (h + 1) * P],
                                                   yz[:, th, h, i * L + t * P:i * L + (t + 1) * P], ident[:])
                last.then_inc(yz_T, 1)
            for k in range(HB):
                for t in range(NT):
                    pe.wait_ge(xh_ready, t + 1)
                    col = (k * NT + t) * P
                    last = nc.tensor.transpose(bank[col // 512][:, col % 512:col % 512 + P],
                                               xh[:, t, k * P:(k + 1) * P], ident[:])
                    if t % 4 == 3:
                        last.then_inc(xh_T, 1)
            pe.wait_ge(xh_c, 4)
            for t in range(NT):
                for k in range(HB):
                    last = nc.tensor.matmul(bank[4][:, t * E:(t + 1) * E], xhT[:, k, t, :], gatew_sb[:, k, :],
                                            start=(k == 0), stop=(k == HB - 1))
            last.then_inc(logits, 1)
            for t in range(NT):
                nc.tensor.matmul(bank[t // 2][:, (t % 2) * H:(t % 2 + 1) * H], ident[:], x_sb[:, t // LB, t % LB, :],
                                 start=(t % 2 == 0), stop=False, skip_group_check=True)
            pe.wait_ge(in_ffn, 32)
            pe.wait_ge(scored, 1)

            def gate_up(e, s0, t):
                s = s0 + t
                if not (isinstance(s, int) and s < 2):
                    pe.wait_ge(hm_ready, s - 1)
                for k in range(HB):
                    w = gu_sb[:, e, k, :] if isinstance(e, int) else \
                        gu_sb[:].rearrange("p e k f -> p (e k f)")[:, bass.ds(e * (HB * 2 * F) + k * 2 * F, 2 * F)]
                    last = nc.tensor.matmul(bank[4 + t % 2][:, 0:2 * F], xhT[:, k, t, :], w,
                                            start=(k == 0), stop=(k == HB - 1))
                last.then_inc(gu_made, 1)

            def turn(s0, t):
                s = s0 + t
                pe.wait_ge(hm_ready, s + 1)
                if not (isinstance(s, int) and s < 2):
                    pe.wait_ge(hT_ready, s - 1)
                nc.tensor.transpose(bank[6 + t % 2][:, 0:P], hm[:, t % 2, :], ident[:]).then_inc(h_T, 1)

            def down(e, s0, t):
                s = s0 + t
                pe.wait_ge(hT_ready, s + 1)
                w = dn_sb[:, e, :] if isinstance(e, int) else \
                    dn_sb[:].rearrange("p e f -> p (e f)")[:, bass.ds(e * H, H)]
                tt = t % NT
                nc.tensor.matmul(bank[tt // 2][:, (tt % 2) * H:(tt % 2 + 1) * H], hT[:, t % 2, :], w,
                                 start=False, stop=True, skip_group_check=True).then_inc(down_done, 1)

            for t in range(NT):
                gate_up(0, 0, t)
                if t >= 1:
                    turn(0, t - 1)
                if t >= 2:
                    down(0, 0, t - 2)
            with pe.Fori(1, E + 1) as e:
                for t in range(NT):
                    gate_up(e, e * NT, t)
                    turn(e * NT, t - 1)
                    down(e if t >= 2 else e - 1, e * NT, t - 2)
            turn((E + 1) * NT, -1)
            down(E, (E + 1) * NT, -2)
            down(E, (E + 1) * NT, -1)


def lay_out(i):
    P = 128

    def blocks(a):
        return np.ascontiguousarray(a.reshape(2, P, -1).transpose(1, 0, 2))

    ctx, w_in, conv_w = i["ctx_1024"], i["L0_xattn_in_proj_w"], i["L0_xattn_conv_w"]
    B, L, DM = ctx.shape
    DI, _, K = conv_w.shape
    ctxT = np.zeros((DM, B, K - 1 + L), ctx.dtype)
    ctxT[:, :, K - 1:] = ctx.transpose(2, 0, 1)
    inwT = np.ascontiguousarray(w_in.T.reshape(DM, 2, P))
    taps = np.ascontiguousarray(conv_w[:, 0, :].reshape(2, P, K).transpose(0, 2, 1))
    xp, dp = i["L0_xattn_x_proj_w"], i["L0_xattn_dt_proj_w"]
    R = dp.shape[1]
    bc = xp[R:]
    projT = blocks(np.concatenate([bc, bc, bc, xp[:R]]).T)
    vecs = [blocks(i[n].reshape(DI, 1)) for n in ("L0_xattn_conv_b", "L0_xattn_dt_proj_b", "L0_xattn_D")]
    dpT = np.zeros((P, DI), dp.dtype)
    dpT[3 * len(bc):3 * len(bc) + R] = dp.T
    parts = [projT, *vecs, blocks(i["L0_xattn_A_log"]), blocks(i["L0_ffn_gate_w"]),
             np.broadcast_to(i["L0_ffn_expert_bias"], (P, 16)), dpT]
    small = np.concatenate([a.reshape(P, -1) for a in parts], axis=1)
    F = i["L0_ffn_shared_gate_w"].shape[1]
    shared = np.concatenate([i["L0_ffn_shared_gate_w"], i["L0_ffn_shared_up_w"]], axis=1)
    gu = np.concatenate([shared[None], i["L0_ffn_experts_gate_up"]])
    gu = np.ascontiguousarray(gu.reshape(-1, 2, P, 2 * F).transpose(2, 0, 1, 3))
    dn = np.concatenate([i["L0_ffn_shared_down_w"][None], i["L0_ffn_experts_down"]])
    dn = np.ascontiguousarray(dn.transpose(1, 0, 2))
    return {"x": i["x"], "ctxT": ctxT, "inwT": inwT, "taps": taps, "small": np.ascontiguousarray(small), "gu": gu, "dn": dn}


def kernel(**inputs):
    import concourse.bacc as _bacc
    from concourse.bass_utils import run_bass_kernel_spmd as _run

    nc = _bacc.Bacc("TRN2", target_bir_lowering=False, num_devices=1)
    arrays, args = {}, []
    for name, a in lay_out({k: np.asarray(v) for k, v in inputs.items()}).items():
        a = np.ascontiguousarray(a)
        arrays[f"in_{name}_dram"] = a
        args.append(nc.dram_tensor(f"in_{name}_dram", a.shape, mybir.dt.from_np(a.dtype), kind="ExternalInput").ap())
    args.append(nc.dram_tensor("out_0_dram", inputs["x"].shape, F32, kind="ExternalOutput").ap())
    block_kernel(nc, *args)
    r = _run(nc, [arrays], core_ids=[0])
    return r.results[0]["out_0_dram"]
```

```python
from contextlib import ExitStack

import concourse.bass as bass
from concourse import mybir
import numpy as np

ALU = mybir.AluOpType
ACT = mybir.ActivationFunctionType
F32 = mybir.dt.float32
BF16 = mybir.dt.bfloat16
U32 = mybir.dt.uint32
AX_X = mybir.AxisListType.X

P = 128
LN2 = 0.6931471805599453
ATANH = (2.0000000012778267, 0.6666639578183403, 0.4002308285536912, 0.27970779753899433, 0.2818452560443701)
C4 = ATANH[4]
FACTORS = [(-r.real, r.imag ** 2) for r in np.roots(ATANH[::-1]) if r.imag > 0]


def block_kernel(nc, x, ctxT_in, inwT_in, taps_in, small_in, gu_in, dn_in, out):
    B, L, H = x.shape
    DM = ctxT_in.shape[0]
    K = taps_in.shape[1]
    E = gu_in.shape[1] - 1
    F = dn_in.shape[0]
    DI, NS, R = 256, 16, 8
    HB = DI // P
    LB = L // P
    NT = B * LB
    BH = 2
    TH = B // BH
    C = BH * L
    NBC = 2 * NS
    NPROJ = 3 * NBC + R
    TOPK = 2
    NJ = E + (TOPK * NT * P - E) // P
    SMALL = small_in.shape[1]
    assert C == 512 and DM == P and F == P and HB == 2 and LB == 2 and H == HB * P and NBC == 32
    EPS = 1e-5
    RING = 12
    BEHIND = 10
    HEAD = (6, 2)
    PE_HEAD = 6
    POOL_HEAD = (8, 2)
    WARM = (14, 12, 16, 0, 12, 4, 4, 5, 2, 0)

    with ExitStack() as stack:
        def sb(name, shape, dt=F32):
            return stack.enter_context(nc.sbuf_tensor(name, shape, dt))

        def sem(name):
            return stack.enter_context(nc.semaphore(name))

        bank = [stack.enter_context(nc.psum_tensor(f"bank{i}", [P, 512], F32)) for i in range(8)]

        ctxT = sb("ctxT", [P, B, K - 1 + L])
        inwT = sb("inwT", [P, HB, P])
        cw_rep = sb("cw_rep", [P, HB, K, P])
        small = sb("small", [P, SMALL])
        x_sb = sb("x_sb", [P, B, LB, H])
        gu_sb = sb("gu_sb", [P, E + 1, HB, 2 * F])
        dn_sb = sb("dn_sb", [P, E + 1, H])

        def view(at, *dims):
            n = int(np.prod(dims))
            v = small[:, at:at + n]
            return v if len(dims) == 1 else v.rearrange(f"p (a b) -> p a b", a=dims[0])
        projT = view(0, HB, NPROJ)
        cb_sb, db_sb, d_sb = (view(HB * NPROJ + i * HB, HB) for i in range(3))
        al_sb = view(HB * NPROJ + 3 * HB, HB, NS)
        gatew_sb = view(HB * NPROJ + 3 * HB + HB * NS, HB, E)
        bias_sb = view(HB * NPROJ + 3 * HB + HB * NS + HB * E, E)
        dpT = small[3 * NBC:NPROJ, SMALL - DI:SMALL].rearrange("r (h q) -> r h q", h=HB)

        ident = sb("ident", [P, P])
        rowsel = sb("rowsel", [3 * NBC, NBC, P], BF16)
        rowsel1 = sb("rowsel1", [3 * NBC, NBC])
        minus_half = sb("minus_half", [P, NT])
        soft_c = sb("soft_c", [P, 3])
        expert_no = sb("expert_no", [P, E])

        wkT = sb("wkT", [P, HB, K, P])
        A_sb = sb("A_sb", [P, HB, NS])
        scan_in = sb("scan_in", [P, 4, TH * HB * C])
        u_sb, dt_sb, dtu_sb, zs_sb = (scan_in[:, i, :].rearrange("p (a h c) -> p a h c", a=TH, h=HB) for i in range(4))
        du_sb = sb("du_sb", [P, TH, HB, C])
        bc3 = sb("bc3", [3 * NBC, TH, C], BF16)
        bc_res = sb("bc_res", [3 * NBC, TH, C])
        dl_sb = sb("dl_sb", [P, TH, C])
        soft = {n: sb(f"soft_{n}", [P, TH, HB, C]) for n in ("abs", "relu", "s", "t", "v")}
        st6 = sb("st6", [P, NT, 6])
        mv = sb("mv", [P, NT, 2])
        ve = sb("ve", [P, NT])
        rstd = sb("rstd", [P, NT])
        nmr = sb("nmr", [P, NT])
        neg_mean = sb("neg_mean", [P, NT // 2])
        brep = sb("brep", [P, 2, C])
        products = sb("products", [P, 2, 2, HB, C])
        dbu = products[:, 0]
        hst = sb("hst", [P, HB, C])
        hc = products[:, 1]
        yz = du_sb

        xh = soft["abs"][:].rearrange("p a h c -> p (a h c)").rearrange("p (t d) -> p t d", t=NT)
        xhT = soft["relu"][:].rearrange("p a h c -> p (a h c)").rearrange("p (k t q) -> p k t q", k=HB, t=NT)
        o_sb = soft["t"][:].rearrange("p a h c -> p (a h c)").rearrange("p (t d) -> p t d", t=NT)
        picked = [soft["s"], soft["v"]]
        rows = scan_in[:].rearrange("p a c -> p (a c)")[:, 0:NJ * H].rearrange("p (j d) -> p j d", j=NJ)
        xh_dram = nc.dram_tensor("xh_dram", [NT * P, H], F32).ap()
        YROWS = (1 + TOPK) * NT * P
        y_dram = nc.dram_tensor("y_dram", [YROWS + NJ * P, H], F32).ap()
        score = sb("score", [P, NT, E])
        biased = sb("biased", [P, NT, E])
        top = sb("top", [P, NT, 8])
        topi = sb("topi", [P, NT, 8], U32)
        topf = sb("topf", [P, TOPK, NT])
        chosen = sb("chosen", [P, TOPK, NT, E])
        both = sb("both", [P, NT, E], BF16)
        prod = sb("prod", [P, TOPK, NT, E])
        raw_w = sb("raw_w", [P, TOPK, NT])
        wsum = sb("wsum", [P, NT])
        winv = sb("winv", [P, NT])
        weight = sb("weight", [P, TOPK, NT])
        before = sb("before", [P, P], BF16)
        ones = sb("ones", [P, P], BF16)
        full = sb("full", [P, E, NT])
        blocks_e = sb("blocks_e", [P, E])
        upto = sb("upto", [P, E])
        base = sb("base", [P, E])
        zeros_e = sb("zeros_e", [P, E])
        slot_e = sb("slot_e", [P, NT, E])
        slot_f = sb("slot_f", [P, TOPK, NT])
        slot_u = sb("slot_u", [P, TOPK, NT], U32)
        slot_lo = sb("slot_lo", [P, TOPK, NT], U32)
        slot_hi = sb("slot_hi", [P, TOPK, NT], U32)
        lo_f = sb("lo_f", [P, TOPK, NT])
        hi_f = sb("hi_f", [P, TOPK, NT])
        count_up = sb("count_up", [P, P])
        block_no = sb("block_no", [P, NT])
        row_no = sb("row_no", [P, 1])
        block_t = sb("block_t", [P, TOPK, NT])
        spare_row = sb("spare_row", [P, 32])
        spare = sb("spare", [P, 32])
        to_f = sb("to_f", [P, 32])
        to_u = sb("to_u", [P, 32], U32)
        from_u = sb("from_u", [P, 32], U32)
        place = wkT[:].rearrange("p h k q -> p (h k q)").bitcast(BF16) \
            .rearrange("p (k t q) -> p k t q", k=TOPK, t=NT)
        taps_flat = cw_rep[:].rearrange("p h k q -> p (h k q)")
        block1 = taps_flat[:, 0:TOPK * NT * 32].rearrange("p (k t j) -> p k t j", k=TOPK, t=NT)
        token_of = taps_flat[:, TOPK * NT * 32:2 * TOPK * NT * 32].bitcast(BF16) \
            .rearrange("p (k t c j) -> p k t c j", k=TOPK, t=NT, c=2)
        ring = products[:].rearrange("p i q h c -> p (i q h c)")[:, 0:RING * H].rearrange("p (g d) -> p g d", d=H)
        past = dl_sb[:, 0, :].rearrange("p (j e) -> p j e", e=E)
        rowsT = hst[:, 0, :].rearrange("p (q k s) -> p q k s", q=2, k=HB)
        hT = hst[:, 1, 0:2 * P].rearrange("p (q s) -> p q s", q=2)
        inv_lo = sb("inv_lo", [P, 32])
        inv_f = sb("inv_f", [P, 32])
        inv_u = sb("inv_u", [P, 32], U32)
        expert_f = sb("expert_f", [P, 32])
        expert_g = sb("expert_g", [P, 32])
        expert_u = sb("expert_u", [P, 32], U32)
        sg = sb("sg", [P, 2, F])
        hm = sb("hm", [P, 2, F])

        in_first = sem("in_first")
        in_small = sem("in_small")
        in_taps = sem("in_taps")
        in_x = sem("in_x")
        in_ffn = sem("in_ffn")
        out_done = sem("out_done")
        ident_zeroed = sem("ident_zeroed")
        ident_ready = sem("ident_ready")
        consts = sem("consts")
        rowsel1_ready = sem("rowsel1_ready")
        rowsel_ready = sem("rowsel_ready")
        taps_ready = sem("taps_ready")
        conv_done = sem("conv_done")
        u_ready = sem("u_ready")
        proj_done = sem("proj_done")
        dl_copied = sem("dl_copied")
        split = sem("split")
        dtp_done = sem("dtp_done")
        soft_act = sem("soft_act")
        abs_ready = sem("abs_ready")
        relu_ready = sem("relu_ready")
        soft_consts = sem("soft_consts")
        soft_dve = sem("soft_dve")
        du_ready = sem("du_ready")
        dtu_ready = sem("dtu_ready")
        bn = sem("bn")
        var_ready = sem("var_ready")
        rstd_ready = sem("rstd_ready")
        nmr_ready = sem("nmr_ready")
        mean_ready = sem("mean_ready")
        z_ready = sem("z_ready")
        a_exp = sem("a_exp")
        a_ready = sem("a_ready")
        decay_zeroed = sem("decay_zeroed")
        brep_made = sem("brep_made")
        brep_copied = sem("brep_copied")
        crep_made = sem("crep_made")
        decay_ready = sem("decay_ready")
        dbu_ready = sem("dbu_ready")
        scanned = sem("scanned")
        hc_ready = sem("hc_ready")
        summed = sem("summed")
        yz_ready = sem("yz_ready")
        yz_T = sem("yz_T")
        x1_ready = sem("x1_ready")
        xh_ready = [sem(f"xh_ready{i}") for i in range(TH)]
        xh_out = sem("xh_out")
        consts_e = sem("consts_e")
        counted = sem("counted")
        inverted = sem("inverted")
        tokens_ready = sem("tokens_ready")
        experts_ready = sem("experts_ready")
        base_ready = sem("base_ready")
        block1_ready = sem("block1_ready")
        token_of_ready = sem("token_of_ready")
        both_ready = sem("both_ready")
        gathered = [sem(f"gathered{i}") for i in range(RING)]
        rows_T = sem("rows_T")
        rowsT_ready = sem("rowsT_ready")
        egu_made = sem("egu_made")
        esilu_done = sem("esilu_done")
        ehm_ready = sem("ehm_ready")
        eh_T = sem("eh_T")
        ehT_ready = sem("ehT_ready")
        edown_done = sem("edown_done")
        y_moved = sem("y_moved")
        y_out = sem("y_out")
        picked_first = [sem(f"picked_first{i}") for i in range(B)]
        picked_second = [sem(f"picked_second{i}") for i in range(B)]
        weights_ready = sem("weights_ready")
        second_weighted = sem("second_weighted")
        targets_ready = sem("targets_ready")
        first_added = sem("first_added")
        xh_T = sem("xh_T")
        xh_c = sem("xh_c")
        logits = sem("logits")
        scored = sem("scored")
        route = sem("route")
        gu_made = sem("gu_made")
        silu_done = sem("silu_done")
        hm_ready = sem("hm_ready")
        h_T = sem("h_T")
        hT_ready = sem("hT_ready")
        down_done = sem("down_done")
        o_base = sem("o_base")
        o_ready = sem("o_ready")

        conv_ps = [bank[4], bank[5], bank[6], bank[7]]
        proj_ps = [bank[0], bank[1]]
        dtp_ps = [bank[2], bank[3], bank[4], bank[5]]
        y_ps = [bank[0], bank[1]]
        b_ps, c_ps = bank[2], bank[3]
        decay_ps = [[bank[6], bank[7]], [bank[4], bank[5]]]
        yT_ps = [bank[6], bank[7], bank[2], bank[3]]
        xhT_ps = [[bank[4], bank[5]], [bank[6], bank[7]]]
        logit_ps = [bank[0], bank[1]]
        NTH = NT // TH

        def picked_rows(k):
            return picked[k][:].rearrange("p a h c -> p (a h c)").rearrange("p (t d) -> p t d", t=NT)

        def fetch_choice(engine, k):
            engine.wait_ge(y_out, 16 * NJ)
            for b in range(B):
                at = (1 + k) * NT * P + b * L
                engine.dma_start(picked_rows(k)[:, b * LB:(b + 1) * LB, :],
                                 y_dram[at:at + L, :].rearrange("(t p) d -> p t d", p=P)).then_inc((picked_first, picked_second)[k][b], 16)

        def act_stage(th, i, h):
            return th * 6 * HB + (HB * i + h + 1 if i < 2 else 2 * HB + 4 * h + i - 1)

        def dve_stage(th, i, h):
            return th * 4 * HB + (h + 1 if i == 0 else HB + 3 * h + i)

        block = stack.enter_context(nc.Block())

        @block.sync
        def _(sp):
            sp.dma_start(ctxT[:], ctxT_in).then_inc(in_first, 16)
            sp.dma_start(cw_rep[:], taps_in.partition_broadcast(P)).then_inc(in_taps, 16)
            sp.dma_start(x_sb[:], x.rearrange("b (t p) d -> p b t d", p=P)).then_inc(in_x, 16)
            sp.dma_start(gu_sb[:], gu_in).then_inc(in_ffn, 16)
            sp.dma_start(dn_sb[:], dn_in).then_inc(in_ffn, 16)
            for th in range(TH):
                sp.wait_ge(xh_ready[th], NTH)
                sp.dma_start(xh_dram[th * NTH * P:(th + 1) * NTH * P, :].rearrange("(t p) d -> p t d", p=P),
                             xh[:, th * NTH:(th + 1) * NTH, :]).then_inc(xh_out, 16)
            fetch_choice(sp, 0)
            for b in range(B):
                sp.wait_ge(o_ready, b + 1)
                sp.dma_start(out[b].rearrange("(t p) d -> p t d", p=P), o_sb[:, b * LB:(b + 1) * LB, :]).then_inc(out_done, 16)
            sp.wait_ge(out_done, 16 * B)

        @block.gpsimd
        def _(pool):
            nc.gpsimd.memset(ident[:], 0.0).then_inc(ident_zeroed, 1)
            nc.gpsimd.memset(minus_half[:], -0.5).then_inc(consts, 1)
            for i, c in enumerate((float(np.log(C4)), FACTORS[0][0], FACTORS[1][0])):
                nc.gpsimd.memset(soft_c[:, i:i + 1], c).then_inc(soft_consts, 1)
            pool.wait_ge(ident_zeroed, 1)
            nc.gpsimd.affine_select(out=ident[:], in_=ident[:], compare_op=ALU.not_equal, fill=1.0, base=0,
                                    pattern=[[-1, P]], channel_multiplier=1).then_inc(ident_ready, 1)
            nc.gpsimd.iota(expert_no[:], [[1, E]], base=0, channel_multiplier=0,
                           allow_small_or_imprecise_dtypes=True).then_inc(consts, 1)
            nc.gpsimd.iota(count_up[:], [[1, P]], base=0, channel_multiplier=0,
                           allow_small_or_imprecise_dtypes=True).then_inc(consts_e, 1)
            nc.gpsimd.iota(block_no[:], [[P, NT]], base=0, channel_multiplier=0,
                           allow_small_or_imprecise_dtypes=True).then_inc(consts_e, 1)
            nc.gpsimd.iota(row_no[:], [[0, 1]], base=0, channel_multiplier=1,
                           allow_small_or_imprecise_dtypes=True).then_inc(consts_e, 1)
            nc.gpsimd.iota(block_t[:], [[NT, TOPK], [1, NT]], base=NT, channel_multiplier=0,
                           allow_small_or_imprecise_dtypes=True).then_inc(consts_e, 1)
            nc.gpsimd.iota(spare_row[:], [[P, 32]], base=YROWS, channel_multiplier=1,
                           allow_small_or_imprecise_dtypes=True).then_inc(consts_e, 1)
            nc.gpsimd.memset(zeros_e[:], 0.0).then_inc(consts_e, 1)
            nc.gpsimd.memset(ones[:], 1.0).then_inc(consts_e, 1)
            pool.wait_ge(consts_e, 7)
            nc.gpsimd.affine_select(out=before[:], in_=ones[:], compare_op=ALU.is_gt, fill=0.0, base=0,
                                    pattern=[[1, P]], channel_multiplier=-1).then_inc(consts_e, 1)
            pool.wait_ge(consts, 1)
            pool.wait_ge(var_ready, 1)
            nc.gpsimd.tensor_tensor(rstd[:], ve[:], minus_half[:], ALU.pow).then_inc(rstd_ready, 1)
            pool.wait_ge(in_small, 16)
            for k in range(TH * HB):
                th, h = divmod(k, HB)
                pool.wait_ge(u_ready, k + 1)
                nc.gpsimd.tensor_scalar(du_sb[:, th, h, :], u_sb[:, th, h, :], d_sb[:, h:h + 1], 1.0,
                                        ALU.mult, ALU.mult).then_inc(du_ready, 1)

            def step_input(th):
                for h in range(HB):
                    pool.wait_ge(soft_dve, dve_stage(th, 3, h))
                    nc.gpsimd.tensor_tensor(dtu_sb[:, th, h, :], dt_sb[:, th, h, :], u_sb[:, th, h, :],
                                            ALU.mult).then_inc(dtu_ready, 1)

            def drive(th, j, q):
                pool.wait_ge(brep_copied, j + 1)
                for h in range(HB):
                    if not (isinstance(j, int) and j < 2):
                        pool.wait_ge(scanned, HB * j - 2 * HB + h + 1)
                    nc.gpsimd.tensor_tensor(dbu[:, q, h, :], dtu_sb[:, th, h, :], brep[:, q, :],
                                            ALU.mult).then_inc(dbu_ready, 1)

            step_input(0)
            for th in range(TH):
                pool.wait_ge(dtu_ready, (th + 1) * HB)
                for n in range(POOL_HEAD[th]):
                    drive(th, th * NS + n, n % 2)
                if th == 0:
                    step_input(1)
                with pool.Fori(POOL_HEAD[th] // 2, NS // 2) as m:
                    for q in range(2):
                        drive(th, m * 2 + (th * NS + q), q)
            for th in range(TH):
                pool.wait_ge(var_ready, th + 2)
                ts = slice(th * NTH, (th + 1) * NTH)
                nc.gpsimd.tensor_tensor(rstd[:, ts], ve[:, ts], minus_half[:, ts], ALU.pow).then_inc(rstd_ready, 1)
                if th == 0:
                    pool.wait_ge(mean_ready, 1)
                    pool.wait_ge(rstd_ready, 2)
                    nc.gpsimd.tensor_tensor(nmr[:, ts], neg_mean[:], rstd[:, ts], ALU.mult).then_inc(nmr_ready, 1)
            tk = token_of.rearrange("p k t c j -> p (k t) c j")
            b1 = block1.rearrange("p k t j -> p (k t) j")
            pool.wait_ge(block1_ready, 1)
            nc.gpsimd.tensor_scalar(tk[:, :, 0, :], b1, row_no[:, 0:1], 1.0, ALU.mult, ALU.mult).then_inc(token_of_ready, 1)
            nc.gpsimd.tensor_tensor(tk[:, :, 1, :], b1, block_t[:].rearrange("p k t -> p (k t)").unsqueeze(2)
                                    .to_broadcast([P, TOPK * NT, 32]), ALU.mult).then_inc(token_of_ready, 1)
            pool.wait_ge(xh_out, 16 * TH)
            pool.wait_ge(tokens_ready, 1)
            for j in range(NJ + BEHIND):
                if j < NJ:
                    if j >= RING:
                        pool.wait_ge(rows_T, j - RING + 1)
                    nc.gpsimd.indirect_dma_start(ring[:, j % RING, :], None, xh_dram,
                                                 bass.IndirectOffsetOnAxis(ap=from_u[:, j:j + 1], axis=0)).then_inc(gathered[j % RING], 16)
                i = j - BEHIND
                if i >= 0:
                    if i == 0:
                        pool.wait_ge(targets_ready, 1)
                    pool.wait_ge(y_moved, i + 1)
                    nc.gpsimd.indirect_dma_start(y_dram, bass.IndirectOffsetOnAxis(ap=to_u[:, i:i + 1], axis=0),
                                                 rows[:, i, :], None).then_inc(y_out, 16)

        @block.scalar
        def _(act):
            act.dma_start(inwT[:], inwT_in).then_inc(in_first, 16)
            act.dma_start(small[:], small_in).then_inc(in_small, 16)

            nc.scalar.preload_act_table(ACT.Silu)

            def make_u(k):
                th, h = divmod(k, HB)
                act.wait_ge(conv_done, k + 1)
                nc.scalar.activation(u_sb[:, th, h, :], conv_ps[k][:], ACT.Silu,
                                     bias=cb_sb[:, h:h + 1]).then_inc(u_ready, 1)

            def make_z(b):
                for h in range(HB):
                    t = b * HB + h
                    nc.scalar.activation(zs_sb[:, b // BH, h, (b % BH) * L:(b % BH + 1) * L], x_sb[:, b, h, :],
                                         ACT.Silu, bias=nmr[:, t:t + 1], scale=rstd[:, t:t + 1]).then_inc(z_ready, 1)
            act.wait_ge(in_small, 16)
            make_u(0)
            make_u(1)
            act.wait_ge(nmr_ready, 1)
            make_z(0)
            make_z(1)
            make_u(2)
            make_z(2)
            make_z(3)
            make_u(3)
            nc.scalar.preload_act_table_set("natural_log_exp_and_others")
            nc.scalar.activation(A_sb[:], al_sb, ACT.Exp).then_inc(a_exp, 1)

            def absolute(th):
                for h in range(HB):
                    act.wait_ge(dtp_done, HB * th + h + 1)
                    nc.scalar.activation(soft["abs"][:, th, h, :], dtp_ps[th * HB + h][:], ACT.Abs,
                                         bias=db_sb[:, h:h + 1]).then_inc(abs_ready, 1)

            def first_exps(th):
                for h in range(HB):
                    act.wait_ge(abs_ready, HB * th + h + 1)
                    nc.scalar.activation(soft["s"][:, th, h, :], soft["abs"][:, th, h, :], ACT.Exp,
                                         scale=-1.0).then_inc(soft_act, 1)
                for h in range(HB):
                    act.wait_ge(soft_act, act_stage(th, 0, h))
                    nc.scalar.activation(soft["t"][:, th, h, :], soft["s"][:, th, h, :], ACT.Ln,
                                         bias=1.0, scale=0.5).then_inc(soft_act, 1)

            def second_exps(th, h):
                w = {n: v[:, th, h, :] for n, v in soft.items()}
                act.wait_ge(soft_dve, dve_stage(th, 0, h))
                nc.scalar.activation(w["s"], w["v"], ACT.Exp, scale=-1.0, bias=soft_c[:, 0:1]).then_inc(soft_act, 1)
                act.wait_ge(soft_act, act_stage(th, 2, h))
                nc.scalar.activation(w["t"], w["s"], ACT.Square, scale=1.0 / C4).then_inc(soft_act, 1)
                act.wait_ge(soft_act, act_stage(th, 3, h))
                nc.scalar.activation(w["abs"], w["t"], ACT.Square, bias=soft_c[:, 1:2]).then_inc(soft_act, 1)
                nc.scalar.activation(w["v"], w["t"], ACT.Square, bias=soft_c[:, 2:3]).then_inc(soft_act, 1)

            act.wait_ge(soft_consts, 3)
            absolute(0)
            first_exps(0)
            for h in range(HB):
                second_exps(0, h)
            absolute(1)

            def decay(th, n, j, q):
                first = isinstance(j, int) and j < 2
                act.wait_ge(brep_made, j + 1)
                if not first:
                    act.wait_ge(dbu_ready, HB * j - HB)
                nc.scalar.copy(brep[:, q, :], b_ps[:]).then_inc(brep_copied, 1)
                if first:
                    act.wait_ge(decay_zeroed, HB * (q + 1))
                for h in range(HB):
                    if not first:
                        act.wait_ge(scanned, HB * j - 2 * HB + h + 1)
                    elif j == 0:
                        act.wait_ge(soft_dve, dve_stage(0, 3, h))
                    v = decay_ps[q][h][:].rearrange("p (b l) -> p b l", b=BH)[:, :, 1:]
                    d = dt_sb[:, th, h, :].rearrange("p (b l) -> p b l", b=BH)[:, :, 1:]
                    nc.scalar.activation(v, d, ACT.Exp, scale=A_sb[:, h, bass.ds(n, 1)]).then_inc(decay_ready, 1)

            act.wait_ge(a_ready, 1)
            for th in range(TH):
                if th >= 1:
                    act.wait_ge(soft_dve, dve_stage(th, 3, HB - 1))
                head = HEAD[th]
                for n in range(head):
                    decay(th, n, th * NS + n, n % 2)
                    if th == 0 and n == 1:
                        first_exps(1)
                    if th == 0 and n in (3, 5):
                        second_exps(1, (n - 3) // 2)
                with act.Fori(head // 2, NS // 2) as m:
                    for q in range(2):
                        decay(th, m * 2 + q, m * 2 + (th * NS + q), q)

            nc.scalar.preload_act_table(ACT.Sigmoid)

            def move_xhT(th):
                for k in range(HB):
                    act.wait_ge(xh_T, HB * th + k + 1)
                    nc.scalar.copy(xhT[:, k, th * NTH:(th + 1) * NTH, :].rearrange("p t q -> p (t q)"),
                                   xhT_ps[th][k][:]).then_inc(xh_c, 1)

            def sigmoid(th):
                act.wait_ge(logits, th + 1)
                nc.scalar.activation(score[:, th * NTH:(th + 1) * NTH, :].rearrange("p t e -> p (t e)"),
                                     logit_ps[th][:, 0:NTH * E], ACT.Sigmoid).then_inc(scored, 1)

            act.wait_ge(nmr_ready, 2)
            for t in range(NTH):
                nc.scalar.activation(xh[:, t, :], x_sb[:, t // LB, t % LB, :], ACT.Identity, bias=nmr[:, t:t + 1],
                                     scale=rstd[:, t:t + 1]).then_inc(xh_ready[0], 1)
            move_xhT(0)
            move_xhT(1)
            sigmoid(0)
            act.wait_ge(xh_ready[1], NTH)
            for b in range(BH, B):
                nc.scalar.copy(x_sb[:, b, :, :], yT_ps[b][:].rearrange("p (t d) -> p t d", t=LB)).then_inc(x1_ready, 1)
            sigmoid(1)
            nc.scalar.preload_act_table(ACT.Silu)

            def gate(t):
                act.wait_ge(gu_made, t + 1)
                if t >= 2:
                    act.wait_ge(hm_ready, t - 1)
                nc.scalar.activation(sg[:, t % 2, :], bank[4 + t % 2][:, 0:F], ACT.Silu).then_inc(silu_done, 1)

            def move_hT(t):
                act.wait_ge(h_T, t + 1)
                if t >= 2:
                    act.wait_ge(down_done, t - 1)
                nc.scalar.copy(hT[:, t % 2, :], bank[6 + t % 2][:, 0:P]).then_inc(hT_ready, 1)

            for t in range(NT):
                gate(t)
                if t >= 1:
                    move_hT(t - 1)
            move_hT(NT - 1)
            def expert_gate(j, q):
                act.wait_ge(egu_made, j + 1)
                if not (isinstance(j, int) and j < 2):
                    act.wait_ge(ehm_ready, j - 1)
                nc.scalar.activation(sg[:, q, :], bank[2 + q][:, 0:F], ACT.Silu).then_inc(esilu_done, 1)

            def expert_hT(j, q):
                act.wait_ge(eh_T, j + 1)
                if not (isinstance(j, int) and j < 2):
                    act.wait_ge(edown_done, j - 1)
                nc.scalar.copy(hT[:, q, :], bank[4 + q][:, 0:P]).then_inc(ehT_ready, 1)

            def expert_y(j, q):
                act.wait_ge(edown_done, j + 1)
                nc.scalar.copy(rows[:, bass.ds(j, 1), :].rearrange("p a d -> p (a d)"), bank[6 + q][:, 0:H]).then_inc(y_moved, 1)

            expert_gate(0, 0)
            expert_gate(1, 1)
            expert_hT(0, 0)
            with act.Fori(1, NJ // 2) as m:
                for q in range(2):
                    expert_gate(m * 2 + q, q)
                    expert_hT(m * 2 + (q - 1), 1 - q)
                    expert_y(m * 2 + (q - 2), q)
            expert_gate(NJ - 1, 0)
            expert_hT(NJ - 2, 1)
            expert_y(NJ - 3, 0)
            expert_hT(NJ - 1, 0)
            expert_y(NJ - 2, 1)
            expert_y(NJ - 1, 0)
            fetch_choice(act, 1)
            act.wait_ge(weights_ready, 1)
            for t in range(NT):
                act.wait_ge(picked_second[t // LB], 16)
                nc.scalar.activation(picked_rows(1)[:, t, :], picked_rows(1)[:, t, :], ACT.Copy,
                                     scale=weight[:, 1, t:t + 1]).then_inc(second_weighted, 1)

        @block.vector
        def _(dve):
            dve.wait_ge(in_first, 32)
            dve.wait_ge(in_taps, 16)
            for h in range(HB):
                nc.vector.tensor_tensor(wkT[:, h, :, :], inwT[:, h, :].unsqueeze(1).to_broadcast([P, K, P]),
                                        cw_rep[:, h, :, :], ALU.mult).then_inc(taps_ready, 1)

            bn_count = [0]

            def x_rows(t):
                return x_sb[:, t // LB, t % LB, :]

            def summed_rows(t):
                return yT_ps[t // LB][:, (t % LB) * H:(t % LB + 1) * H]

            def stats(ts, of=x_rows):
                for t in ts:
                    nc.vector.bn_stats(st6[:, t, :], of(t)).then_inc(bn, 1)
                for i, t in enumerate(ts):
                    dve.wait_ge(bn, bn_count[0] + i + 1)
                    nc.vector.bn_aggr(mv[:, t, :], st6[:, t, :]).then_inc(bn, 1)
                bn_count[0] += 2 * len(ts)
                dve.wait_ge(bn, bn_count[0])
                nc.vector.tensor_scalar(ve[:, ts[0]:ts[-1] + 1], mv[:, ts[0]:ts[-1] + 1, 1], EPS, None,
                                        ALU.add).then_inc(var_ready, 1)

            dve.wait_ge(in_x, 16)
            stats(range(NT))
            dve.wait_ge(ident_ready, 1)
            idn = [ident[0:3 * NBC, q * NBC:(q + 1) * NBC] for q in range(3)]
            nc.vector.tensor_tensor(rowsel1[:], idn[0], idn[1], ALU.add).then_inc(rowsel1_ready, 1)
            dve.wait_ge(rowsel1_ready, 1)
            nc.vector.tensor_tensor(rowsel1[:], rowsel1[:], idn[2], ALU.add).then_inc(rowsel1_ready, 1)
            dve.wait_ge(rstd_ready, 1)
            nc.vector.scalar_tensor_tensor(out=nmr[:], in0=mv[:, :, 0], scalar=-1.0, in1=rstd[:],
                                           op0=ALU.mult, op1=ALU.mult).then_inc(nmr_ready, 1)
            dve.wait_ge(rowsel1_ready, 2)
            nc.vector.tensor_copy(rowsel[:], rowsel1[:].unsqueeze(2).to_broadcast([3 * NBC, NBC, P])).then_inc(rowsel_ready, 1)

            def copy_dl(th):
                dve.wait_ge(proj_done, th + 1)
                nc.vector.tensor_copy(dl_sb[3 * NBC:NPROJ, th, :], proj_ps[th][3 * NBC:NPROJ, :]).then_inc(dl_copied, 1)

            def split_bc(th):
                X = proj_ps[th][0:3 * NBC, :]
                c = 5 * th
                nc.vector.tensor_copy(bc3[:, th, :], X).then_inc(split, 1)
                dve.wait_ge(split, c + 1)
                nc.vector.tensor_tensor(bc_res[:, th, :], X, bc3[:, th, :], ALU.subtract).then_inc(split, 1)
                dve.wait_ge(split, c + 2)
                for q in (1, 2):
                    rows = slice(q * NBC, (q + 1) * NBC)
                    nc.vector.tensor_copy(bc3[rows, th, :], bc_res[rows, th, :]).then_inc(split, 1)
                dve.wait_ge(split, c + 4)
                nc.vector.tensor_tensor(bc3[rows, th, :], bc_res[rows, th, :], bc3[rows, th, :],
                                        ALU.subtract).then_inc(split, 1)

            def relu(th):
                for h in range(HB):
                    dve.wait_ge(abs_ready, HB * th + h + 1)
                    nc.vector.tensor_scalar(soft["relu"][:, th, h, :], dtp_ps[th * HB + h][:], db_sb[:, h:h + 1], 0.0,
                                            ALU.add, ALU.max).then_inc(relu_ready, 1)

            def exponents(th):
                for h in range(HB):
                    dve.wait_ge(soft_act, act_stage(th, 1, h))
                    nc.vector.scalar_tensor_tensor(out=soft["v"][:, th, h, :], in0=soft["abs"][:, th, h, :], scalar=LN2,
                                                   in1=soft["t"][:, th, h, :], op0=ALU.add, op1=ALU.add).then_inc(soft_dve, 1)

            def step_size(th, h):
                w = {n: v[:, th, h, :] for n, v in soft.items()}
                dve.wait_ge(soft_act, act_stage(th, 5, h))
                for i, (n, m, (_, d)) in enumerate((("v", "s", FACTORS[1]), ("abs", "v", FACTORS[0]))):
                    nc.vector.scalar_tensor_tensor(out=w["v"], in0=w[n], scalar=d, in1=w[m],
                                                   op0=ALU.add, op1=ALU.mult).then_inc(soft_dve, 1)
                    dve.wait_ge(soft_dve, dve_stage(th, i + 1, h))
                dve.wait_ge(relu_ready, HB * th + h + 1)
                nc.vector.tensor_tensor(dt_sb[:, th, h, :], w["v"], w["relu"], ALU.add).then_inc(soft_dve, 1)

            def zero_decays(q):
                for h in range(HB):
                    nc.vector.memset(decay_ps[q][h][:].rearrange("p (b l) -> p b l", b=BH)[:, :, 0:1],
                                     0.0).then_inc(decay_zeroed, 1)

            copy_dl(0)
            split_bc(0)
            relu(0)
            dve.wait_ge(u_ready, TH * HB)
            zero_decays(0)
            copy_dl(1)
            dve.wait_ge(a_exp, 1)
            nc.vector.tensor_scalar(A_sb[:], A_sb[:], -1.0, None, ALU.mult).then_inc(a_ready, 1)
            exponents(0)
            split_bc(1)
            step_size(0, 0)
            step_size(0, 1)
            relu(1)
            dve.wait_ge(relu_ready, HB * TH)
            zero_decays(1)

            def scan(j, q):
                first = isinstance(j, int) and j < 2
                for h in range(HB):
                    dve.wait_ge(decay_ready, HB * j + h + 1)
                    dve.wait_ge(dbu_ready, HB * j + h + 1)
                    if not (isinstance(j, int) and j == 0):
                        dve.wait_ge(hc_ready, HB * j - HB + h + 1)
                    nc.vector.tensor_tensor_scan(hst[:, h, :], decay_ps[q][h][:], dbu[:, q, h, :], 0.0,
                                                 ALU.mult, ALU.add).then_inc(scanned, 1)
                dve.wait_ge(crep_made, j + 1)
                for h in range(HB):
                    dve.wait_ge(scanned, HB * j + h + 1)
                    if not first:
                        dve.wait_ge(summed, HB * j - 2 * HB + h + 1)
                    nc.vector.tensor_tensor(hc[:, q, h, :], hst[:, h, :], c_ps[:], ALU.mult).then_inc(hc_ready, 1)

            def gate_y(th):
                dve.wait_ge(z_ready, NT)
                dve.wait_ge(summed, HB * NS * (th + 1))
                for h in range(HB):
                    nc.vector.tensor_tensor(yz[:, th, h, :], y_ps[h][:], zs_sb[:, th, h, :], ALU.mult).then_inc(yz_ready, 1)

            for th in range(TH):
                scan(th * NS, 0)
                if th >= 1:
                    gate_y(th - 1)
                for n in range(1, HEAD[th]):
                    scan(th * NS + n, n % 2)
                    if th == 0 and n == 1:
                        exponents(1)
                    if th == 0 and n in (3, 5):
                        step_size(1, (n - 3) // 2)
                with dve.Fori(HEAD[th] // 2, NS // 2) as m:
                    for q in range(2):
                        scan(m * 2 + (th * NS + q), q)
            def residual(b):
                dve.wait_ge(yz_T, b + 1)
                xv = x_sb[:, b, :, :]
                nc.vector.tensor_tensor(xv, yT_ps[b][:].rearrange("p (t d) -> p t d", t=LB), xv, ALU.add).then_inc(x1_ready, 1)

            def norm(ts):
                for t in ts:
                    dve.wait_ge(rstd_ready, t // NTH + 2)
                    nc.vector.tensor_scalar(xh[:, t, :], summed_rows(t), mv[:, t, 0:1], rstd[:, t:t + 1],
                                            ALU.subtract, ALU.mult).then_inc(xh_ready[1], 1)

            for b in range(BH):
                residual(b)
            dve.wait_ge(x1_ready, BH)
            gate_y(TH - 1)
            stats(range(NTH))
            nc.vector.tensor_scalar(neg_mean[:], mv[:, 0:NTH, 0], -1.0, None, ALU.mult).then_inc(mean_ready, 1)
            for b in range(BH, B):
                dve.wait_ge(yz_T, b + 1)
            stats(range(NTH, NT), summed_rows)
            norm(range(NTH, NT))
            step = [0]

            def link(ins):
                step[0] += 1
                ins.then_inc(route, 1)
                dve.wait_ge(route, step[0])

            def shared(t):
                dve.wait_ge(silu_done, t + 1)
                if t >= 2:
                    dve.wait_ge(h_T, t - 1)
                nc.vector.tensor_tensor(hm[:, t % 2, :], bank[4 + t % 2][:, F:2 * F], sg[:, t % 2, :],
                                        ALU.mult).then_inc(hm_ready, 1)

            for th in range(TH):
                ts = slice(th * NTH, (th + 1) * NTH)
                dve.wait_ge(scored, th + 1)
                link(nc.vector.tensor_tensor(biased[:, ts], score[:, ts], bias_sb.unsqueeze(1).to_broadcast([P, NTH, E]), ALU.add))
                for t in range(ts.start, ts.stop):
                    nc.vector.max(top[:, t, :], biased[:, t, :]).then_inc(route, 1)
                step[0] += NTH
                for t in range(ts.start, ts.stop):
                    dve.wait_ge(route, step[0] - ts.stop + t + 1)
                    nc.vector.max_index(topi[:, t, :], top[:, t, :], biased[:, t, :]).then_inc(route, 1)
                step[0] += NTH
                dve.wait_ge(route, step[0])
                link(nc.vector.tensor_copy(topf[:, :, ts], topi[:, ts, 0:TOPK].rearrange("p t k -> p k t")))
                for k in range(TOPK):
                    nc.vector.tensor_tensor(chosen[:, k, ts], expert_no[:].unsqueeze(1).to_broadcast([P, NTH, E]),
                                            topf[:, k, ts].unsqueeze(2).to_broadcast([P, NTH, E]), ALU.is_equal).then_inc(route, 1)
                step[0] += TOPK
                dve.wait_ge(route, step[0])
                nc.vector.tensor_tensor(both[:, ts], chosen[:, 0, ts], chosen[:, 1, ts], ALU.add).then_inc(both_ready, 1)
            flat = chosen[:].rearrange("p k t e -> p k (t e)")
            pflat = prod[:].rearrange("p k t e -> p k (t e)")
            dve.wait_ge(counted, 1)
            cnt = bank[3][:, NT * E:NT * E + E]
            link(nc.vector.tensor_tensor(full[:], cnt.unsqueeze(2).to_broadcast([P, E, NT]),
                                         block_no[:].unsqueeze(1).to_broadcast([P, E, NT]), ALU.is_gt))
            link(nc.vector.tensor_reduce(blocks_e[:], full[:], AX_X, ALU.add))
            shared(0)
            link(nc.vector.tensor_tensor_scan(upto[:], blocks_e[:], zeros_e[:], 0.0, ALU.add, ALU.add))
            link(nc.vector.tensor_tensor(base[:], upto[:], blocks_e[:], ALU.subtract))
            link(nc.vector.scalar_tensor_tensor(out=slot_e[:], in0=base[:].unsqueeze(1).to_broadcast([P, NT, E]),
                                                scalar=float(P), in1=bank[3][:, 0:NT * E].rearrange("p (t e) -> p t e", t=NT),
                                                op0=ALU.mult, op1=ALU.add))
            link(nc.vector.tensor_tensor(pflat, flat, slot_e[:].rearrange("p t e -> p (t e)").unsqueeze(1)
                                         .to_broadcast([P, TOPK, NT * E]), ALU.mult))
            link(nc.vector.tensor_reduce(slot_f[:], prod[:], AX_X, ALU.add))
            link(nc.vector.tensor_copy(slot_u[:], slot_f[:]))
            shared(1)
            link(nc.vector.tensor_scalar(slot_hi[:], slot_u[:], 7, None, ALU.logical_shift_right))
            link(nc.vector.tensor_scalar(slot_lo[:], slot_u[:], P - 1, None, ALU.bitwise_and))
            link(nc.vector.tensor_copy(hi_f[:], slot_hi[:]))
            link(nc.vector.tensor_copy(lo_f[:], slot_lo[:]))
            lo = lo_f[:].rearrange("p k t -> p (k t)").unsqueeze(2).to_broadcast([P, TOPK * NT, P])
            hi = hi_f[:].rearrange("p k t -> p (k t)").unsqueeze(2).to_broadcast([P, TOPK * NT, 32])
            nc.vector.tensor_tensor(block1.rearrange("p k t j -> p (k t) j"),
                                    count_up[:, 0:32].unsqueeze(1).to_broadcast([P, TOPK * NT, 32]), hi,
                                    ALU.is_equal).then_inc(block1_ready, 1)
            shared(2)
            for k in range(TOPK):
                nc.vector.tensor_tensor(place[:, k], count_up[:].unsqueeze(1).to_broadcast([P, NT, P]),
                                        lo_f[:, k, :].unsqueeze(2).to_broadcast([P, NT, P]), ALU.is_equal).then_inc(base_ready, 1)
                if k == 0:
                    shared(3)
            link(nc.vector.tensor_tensor(past, upto[:].unsqueeze(1).to_broadcast([P, 32, E]),
                                         count_up[:, 0:32].unsqueeze(2).to_broadcast([P, 32, E]), ALU.is_le))
            shared(4)
            dve.wait_ge(inverted, 1)
            link(nc.vector.tensor_copy(inv_lo[:], bank[3][:, 256:256 + 32]))
            link(nc.vector.scalar_tensor_tensor(out=inv_f[:], in0=bank[3][:, 256 + 32:256 + 64], scalar=float(P), in1=inv_lo[:],
                                                op0=ALU.mult, op1=ALU.add))
            link(nc.vector.tensor_copy(inv_u[:], inv_f[:]))
            nc.vector.tensor_scalar(from_u[:], inv_u[:], NT * P - 1, None, ALU.bitwise_and).then_inc(tokens_ready, 1)
            link(nc.vector.tensor_reduce(expert_f[:], past, AX_X, ALU.add))
            link(nc.vector.tensor_scalar(expert_g[:], expert_f[:], float(E - 1), 1.0, ALU.min, ALU.add))
            nc.vector.tensor_copy(expert_u[:], expert_g[:]).then_inc(experts_ready, 1)
            shared(5)

            def open_o(i):
                dve.wait_ge(x1_ready, B)
                dve.wait_ge(down_done, 2 * i + 2)
                nc.vector.tensor_tensor(o_sb.rearrange("p t d -> p (t d)")[:, i * 512:(i + 1) * 512], bank[i][:],
                                        x_sb[:].rearrange("p b t d -> p (b t d)")[:, i * 512:(i + 1) * 512],
                                        ALU.add).then_inc(o_base, 1)

            open_o(0)
            shared(6)
            open_o(1)
            shared(7)
            open_o(2)
            open_o(3)
            link(nc.vector.scalar_tensor_tensor(out=spare[:], in0=inv_f[:], scalar=1.0, in1=spare_row[:],
                                                op0=ALU.is_lt, op1=ALU.mult))
            link(nc.vector.tensor_tensor(to_f[:], spare[:], inv_f[:], ALU.add))
            nc.vector.tensor_copy(to_u[:], to_f[:]).then_inc(targets_ready, 1)

            def move_rows(j, q):
                dve.wait_ge(rows_T, j + 1)
                if not (isinstance(j, int) and j < 2):
                    dve.wait_ge(egu_made, j - 1)
                nc.vector.tensor_copy(rowsT[:, q, :, :], bank[q][:, 0:H].rearrange("p (k s) -> p k s", k=HB)).then_inc(rowsT_ready, 1)

            def expert_gated(j, q):
                dve.wait_ge(esilu_done, j + 1)
                if not (isinstance(j, int) and j < 2):
                    dve.wait_ge(eh_T, j - 1)
                nc.vector.tensor_tensor(hm[:, q, :], bank[2 + q][:, F:2 * F], sg[:, q, :], ALU.mult).then_inc(ehm_ready, 1)

            move_rows(0, 0)
            for j in range(2):
                move_rows(j + 1, 1 - j)
                expert_gated(j, j)
            with dve.Fori(1, NJ // 2) as m:
                for q in range(2):
                    move_rows(m * 2 + (q + 1), 1 - q)
                    expert_gated(m * 2 + q, q)
            expert_gated(NJ - 1, 0)

            link(nc.vector.tensor_tensor(pflat, flat, score[:].rearrange("p t e -> p (t e)").unsqueeze(1)
                                         .to_broadcast([P, TOPK, NT * E]), ALU.mult))
            link(nc.vector.tensor_reduce(raw_w[:], prod[:], AX_X, ALU.add))
            link(nc.vector.tensor_tensor(wsum[:], raw_w[:, 0, :], raw_w[:, 1, :], ALU.add))
            link(nc.vector.tensor_scalar(wsum[:], wsum[:], 1e-20, None, ALU.add))
            link(nc.vector.reciprocal(winv[:], wsum[:]))
            nc.vector.tensor_tensor(weight[:], raw_w[:], winv[:].unsqueeze(1).to_broadcast([P, TOPK, NT]),
                                    ALU.mult).then_inc(weights_ready, 1)
            dve.wait_ge(weights_ready, 1)
            dve.wait_ge(o_base, 4)
            for t in range(NT):
                dve.wait_ge(picked_first[t // LB], 16)
                nc.vector.scalar_tensor_tensor(out=o_sb[:, t, :], in0=picked_rows(0)[:, t, :], scalar=weight[:, 0, t:t + 1],
                                               in1=o_sb[:, t, :], op0=ALU.mult, op1=ALU.add).then_inc(first_added, 1)
                if t % LB == LB - 1:
                    ts = slice(t + 1 - LB, t + 1)
                    dve.wait_ge(first_added, t + 1)
                    dve.wait_ge(second_weighted, t + 1)
                    nc.vector.tensor_tensor(o_sb[:, ts, :], o_sb[:, ts, :], picked_rows(1)[:, ts, :],
                                            ALU.add).then_inc(o_ready, 1)

        @block.tensor
        def _(pe):
            def conv(k):
                th, h = divmod(k, HB)
                pe.wait_ge(taps_ready, h + 1)
                for i in range(K):
                    last = nc.tensor.matmul(conv_ps[k][:], wkT[:, h, i, :], ctxT[:, th * BH:(th + 1) * BH, i:i + L],
                                            start=(i == 0), stop=(i == K - 1))
                last.then_inc(conv_done, 1)

            def proj(th):
                pe.wait_ge(u_ready, (th + 1) * HB)
                for h in range(HB):
                    last = nc.tensor.matmul(proj_ps[th][0:NPROJ, :], projT[:, h, :], u_sb[:, th, h, :],
                                            start=(h == 0), stop=(h == HB - 1))
                last.then_inc(proj_done, 1)

            def steps(th):
                pe.wait_ge(dl_copied, th + 1)
                for h in range(HB):
                    nc.tensor.matmul(dtp_ps[th * HB + h][:], dpT[:, h, :], dl_sb[3 * NBC:NPROJ, th, :],
                                     start=True, stop=True).then_inc(dtp_done, 1)

            pe.wait_ge(ident_ready, 1)
            def keep_warm(at, n):
                for _ in range(n):
                    nc.tensor.matmul(at[:, 0:P], ident[:], ident[:], start=True, stop=True)

            keep_warm(c_ps, WARM[0])
            pe.wait_ge(in_first, 32)
            conv(0)
            conv(1)
            conv(2)
            pe.wait_ge(in_small, 16)
            proj(0)
            conv(3)
            steps(0)
            proj(1)
            steps(1)

            def spread_b(th, n, j):
                if not (isinstance(j, int) and j == 0):
                    pe.wait_ge(brep_copied, j)
                nc.tensor.matmul(b_ps[:], sel(n), bc3[:, th, :], start=True, stop=True).then_inc(brep_made, 1)

            def spread_c(th, n, j):
                if not (isinstance(j, int) and j == 0):
                    pe.wait_ge(hc_ready, HB * j)
                nc.tensor.matmul(c_ps[:], sel(n + NS), bc3[:, th, :], start=True, stop=True).then_inc(crep_made, 1)

            def sel(m):
                return rowsel[:, m, :] if isinstance(m, int) else \
                    rowsel[:].rearrange("r n q -> r (n q)")[:, bass.ds(m * P, P)]

            def add_state(j, q, opens=False):
                for h in range(HB):
                    nc.tensor.matmul(y_ps[h][:], ident[:], hc[:, q, h, :], start=opens, stop=False,
                                     skip_group_check=True).then_inc(summed, 1)

            def add_du(th, h):
                pe.wait_ge(du_ready, HB * th + h + 1)
                nc.tensor.matmul(y_ps[h][:], ident[:], du_sb[:, th, h, :], start=False, stop=False, skip_group_check=True)

            pe.wait_ge(rowsel_ready, 1)
            pe.wait_ge(split, 5)
            pe.wait_ge(relu_ready, HB)
            pe.wait_ge(abs_ready, HB)
            spread_b(0, 0, 0)
            keep_warm(y_ps[0], WARM[1])
            for th in range(TH):
                j0 = th * NS
                spread_b(th, 1, j0 + 1)
                spread_c(th, 0, j0)
                if th >= 1:
                    add_state(j0 - 1, 1)
                if th == 0:
                    keep_warm(y_ps[0], WARM[2])
                for n in range(1, PE_HEAD):
                    spread_b(th, n + 1, j0 + n + 1)
                    spread_c(th, n, j0 + n)
                    if n == 1 and th >= 1:
                        pe.wait_ge(yz_ready, HB * th)
                    elif n == 1:
                        pe.wait_ge(split, 5 * TH)
                    add_state(j0 + n - 1, (n - 1) % 2, opens=(n == 1))
                    if n in (3, 5):
                        add_du(th, (n - 3) // 2)
                with pe.Fori(PE_HEAD // 2, NS // 2 - 1) as m:
                    for q in range(2):
                        n = m * 2 + q
                        spread_b(th, n + 1, n + (j0 + 1))
                        spread_c(th, n, n + j0)
                        add_state(n + (j0 - 1), 1 - q)
                spread_b(th, NS - 1, j0 + NS - 1)
                spread_c(th, NS - 2, j0 + NS - 2)
                add_state(j0 + NS - 3, 1)
                if th + 1 < TH:
                    spread_b(th + 1, 0, j0 + NS)
                spread_c(th, NS - 1, j0 + NS - 1)
                add_state(j0 + NS - 2, 0)
            def turn_y(b):
                th, i = divmod(b, BH)
                for t in range(LB):
                    for h in range(HB):
                        last = nc.tensor.transpose(yT_ps[b][:, t * H + h * P:t * H + (h + 1) * P],
                                                   yz[:, th, h, i * L + t * P:i * L + (t + 1) * P], ident[:])
                last.then_inc(yz_T, 1)

            for b in range(BH):
                turn_y(b)
            pe.wait_ge(hc_ready, TH * NS * HB)
            add_state(TH * NS - 1, 1)
            keep_warm(xhT_ps[0][1], WARM[3])
            pe.wait_ge(brep_copied, TH * NS)
            for b in range(BH, B):
                nc.tensor.matmul(yT_ps[b][:], ident[:], x_sb[:, b, :, :], start=True, stop=False, skip_group_check=True)
            for h in range(HB):
                pe.wait_ge(yz_ready, HB * (TH - 1) + h + 1)
                for b in range(BH, B):
                    for t in range(LB):
                        col = (b - BH) * L + t * P
                        last = nc.tensor.matmul(yT_ps[b][:, t * H + h * P:t * H + (h + 1) * P], yz[:, TH - 1, h, col:col + P],
                                                ident[:], start=False, stop=(h == HB - 1), skip_group_check=True)
                    if h == HB - 1:
                        last.then_inc(yz_T, 1)

            def turn_xh(th):
                for t in range(th * NTH, (th + 1) * NTH):
                    pe.wait_ge(xh_ready[th], t % NTH + 1)
                    for k in range(HB):
                        last = nc.tensor.transpose(xhT_ps[th][k][:, (t % NTH) * P:(t % NTH + 1) * P],
                                                   xh[:, t, k * P:(k + 1) * P], ident[:])
                        if t % NTH == NTH - 1:
                            last.then_inc(xh_T, 1)

            def router(th):
                pe.wait_ge(xh_c, HB * (th + 1))
                for t in range(NTH):
                    for k in range(HB):
                        last = nc.tensor.matmul(logit_ps[th][:, t * E:(t + 1) * E], xhT[:, k, th * NTH + t, :], gatew_sb[:, k, :],
                                                start=(k == 0), stop=(k == HB - 1))
                last.then_inc(logits, 1)

            keep_warm(xhT_ps[0][0], WARM[4])
            turn_xh(0)
            turn_xh(1)
            router(0)
            keep_warm(logit_ps[1], WARM[5])
            router(1)
            keep_warm(bank[6], WARM[9])
            pe.wait_ge(in_ffn, 32)

            def gate_up(t):
                if t >= 2:
                    pe.wait_ge(hm_ready, t - 1)
                for k in range(HB):
                    last = nc.tensor.matmul(bank[4 + t % 2][:, 0:2 * F], xhT[:, k, t, :], gu_sb[:, 0, k, :],
                                            start=(k == 0), stop=(k == HB - 1))
                last.then_inc(gu_made, 1)

            def turn(t):
                pe.wait_ge(hm_ready, t + 1)
                if t >= 2:
                    pe.wait_ge(hT_ready, t - 1)
                nc.tensor.transpose(bank[6 + t % 2][:, 0:P], hm[:, t % 2, :], ident[:]).then_inc(h_T, 1)

            def down(t):
                pe.wait_ge(hT_ready, t + 1)
                nc.tensor.matmul(bank[t // 2][:, (t % 2) * H:(t % 2 + 1) * H], hT[:, t % 2, :], dn_sb[:, 0, :],
                                 start=True, stop=True).then_inc(down_done, 1)

            def count():
                pe.wait_ge(both_ready, TH)
                pe.wait_ge(x1_ready, B)
                pe.wait_ge(consts_e, 8)
                bf = both[:].rearrange("p t e -> p (t e)")
                at = bank[3]
                nc.tensor.matmul(at[:, 0:NT * E], before[:], bf, start=True, stop=False, skip_group_check=True)
                for t in range(NT):
                    rest = NT - 1 - t
                    if rest:
                        nc.tensor.matmul(at[:, (t + 1) * E:NT * E], ones[:], both[:, t:t + 1, :].to_broadcast([P, rest, E]),
                                         start=False, stop=False, skip_group_check=True)
                    last = nc.tensor.matmul(at[:, NT * E:NT * E + E], ones[:], both[:, t, :],
                                            start=False, stop=(t == NT - 1), skip_group_check=True)
                last.then_inc(counted, 1)

            def invert():
                pe.wait_ge(token_of_ready, 2)
                for i in range(TOPK * NT):
                    k, t = divmod(i, NT)
                    if t == 0:
                        pe.wait_ge(base_ready, k + 1)
                    last = nc.tensor.matmul(bank[3][:, 256:256 + 64], place[:, k, t, :],
                                            token_of[:, k, t, :, :].rearrange("p c j -> p (c j)"),
                                            start=(i == 0), stop=(i == TOPK * NT - 1))
                last.then_inc(inverted, 1)

            gate_up(0)
            keep_warm(bank[6], WARM[6])
            count()
            gate_up(1)
            keep_warm(bank[0], WARM[7])
            turn(0)
            gate_up(2)
            turn(1)
            down(0)
            gate_up(3)
            turn(2)
            down(1)
            gate_up(4)
            turn(3)
            down(2)
            gate_up(5)
            invert()
            turn(4)
            down(3)
            for t in range(6, NT):
                gate_up(t)
                turn(t - 1)
                down(t - 2)
            turn(NT - 1)
            pe.wait_ge(tokens_ready, 1)
            down(NT - 2)
            down(NT - 1)

            keep_warm(bank[6], WARM[8])
            pe.wait_ge(experts_ready, 1)

            before_last, last_one, current, upcoming = \
                (nc.tensor.alloc_register(n) for n in ("expert_before_last", "expert_last", "expert_current", "expert_upcoming"))

            def shift_experts(j):
                nc.tensor.reg_mov(before_last, last_one)
                nc.tensor.reg_mov(last_one, current)
                nc.tensor.reg_mov(current, upcoming)

            def load_upcoming(j):
                nc.tensor.reg_load(upcoming, expert_u[0:1, bass.ds(j, 1)])

            def turn_rows(j, q, g, n):
                if isinstance(j, int) and j < 2:
                    pe.wait_ge(o_base, j + 1)
                pe.wait_ge(gathered[g], n)
                if not (isinstance(j, int) and j < 2):
                    pe.wait_ge(rowsT_ready, j - 1)
                for k in range(HB):
                    last = nc.tensor.transpose(bank[q][:, k * P:(k + 1) * P],
                                               ring[:, g, k * P:(k + 1) * P], ident[:])
                last.then_inc(rows_T, 1)

            def expert_gate_up(j, q):
                e = nc.tensor.snap(current, min_val=1, max_val=E)
                pe.wait_ge(rowsT_ready, j + 1)
                if isinstance(j, int) and j < 2:
                    pe.wait_ge(o_base, j + 3)
                if not (isinstance(j, int) and j < 2):
                    pe.wait_ge(ehm_ready, j - 1)
                for k in range(HB):
                    last = nc.tensor.matmul(bank[2 + q][:, 0:2 * F], rowsT[:, q, k, :],
                                            gu_sb[:].rearrange("p e k f -> p (e k f)")[:, bass.ds(e * (HB * 2 * F) + k * 2 * F, 2 * F)],
                                            start=(k == 0), stop=(k == HB - 1))
                last.then_inc(egu_made, 1)

            def expert_turn(j, q):
                pe.wait_ge(ehm_ready, j + 1)
                if not (isinstance(j, int) and j < 2):
                    pe.wait_ge(ehT_ready, j - 1)
                nc.tensor.transpose(bank[4 + q][:, 0:P], hm[:, q, :], ident[:]).then_inc(eh_T, 1)

            def expert_down(j, q):
                e = nc.tensor.snap(before_last, min_val=1, max_val=E)
                pe.wait_ge(ehT_ready, j + 1)
                if not (isinstance(j, int) and j < 2):
                    pe.wait_ge(y_moved, j - 1)
                nc.tensor.matmul(bank[6 + q][:, 0:H], hT[:, q, :],
                                 dn_sb[:].rearrange("p e f -> p (e f)")[:, bass.ds(e * H, H)],
                                 start=True, stop=True).then_inc(edown_done, 1)

            def step(j, i, n):
                shift_experts(j)
                if not isinstance(j, int) or j + 1 < NJ:
                    turn_rows(j + 1, (i + 1) % 2, (i + 1) % RING, n)
                if not isinstance(j, int) or j < NJ:
                    expert_gate_up(j, i % 2)
                    load_upcoming(j + 1)
                if not isinstance(j, int) or 1 <= j < NJ + 1:
                    expert_turn(j - 1, (i - 1) % 2)
                if not isinstance(j, int) or j >= 2:
                    expert_down(j - 2, i % 2)

            load_upcoming(0)
            for register in (last_one, current):
                nc.tensor.reg_mov(register, upcoming)
            turn_rows(0, 0, 0, 16)
            for j in range(4):
                step(j, j, 16)
            rounds = (NJ - 4) // RING
            with pe.Fori(0, rounds) as m:
                for i in range(4, RING + 4):
                    step(m * RING + i, i % RING, m * 16 + 16 * ((i + 1) // RING + 1))
            for j in range(rounds * RING + 4, NJ + 2):
                step(j, j % RING, 16 * ((j + 1) // RING + 1))


def lay_out(i):
    P = 128

    def blocks(a):
        return np.ascontiguousarray(a.reshape(2, P, -1).transpose(1, 0, 2))

    ctx, w_in, conv_w = i["ctx_1024"], i["L0_xattn_in_proj_w"], i["L0_xattn_conv_w"]
    B, L, DM = ctx.shape
    DI, _, K = conv_w.shape
    ctxT = np.zeros((DM, B, K - 1 + L), ctx.dtype)
    ctxT[:, :, K - 1:] = ctx.transpose(2, 0, 1)
    inwT = np.ascontiguousarray(w_in.T.reshape(DM, 2, P))
    taps = np.ascontiguousarray(conv_w[:, 0, :].reshape(2, P, K).transpose(0, 2, 1))
    xp, dp = i["L0_xattn_x_proj_w"], i["L0_xattn_dt_proj_w"]
    R = dp.shape[1]
    bc = xp[R:]
    projT = blocks(np.concatenate([bc, bc, bc, xp[:R]]).T)
    vecs = [blocks(i[n].reshape(DI, 1)) for n in ("L0_xattn_conv_b", "L0_xattn_dt_proj_b", "L0_xattn_D")]
    dpT = np.zeros((P, DI), dp.dtype)
    dpT[3 * len(bc):3 * len(bc) + R] = dp.T
    parts = [projT, *vecs, blocks(i["L0_xattn_A_log"]), blocks(i["L0_ffn_gate_w"]),
             np.broadcast_to(i["L0_ffn_expert_bias"], (P, 16)), dpT]
    small = np.concatenate([a.reshape(P, -1) for a in parts], axis=1)
    F = i["L0_ffn_shared_gate_w"].shape[1]
    shared = np.concatenate([i["L0_ffn_shared_gate_w"], i["L0_ffn_shared_up_w"]], axis=1)
    gu = np.concatenate([shared[None], i["L0_ffn_experts_gate_up"]])
    gu = np.ascontiguousarray(gu.reshape(-1, 2, P, 2 * F).transpose(2, 0, 1, 3))
    dn = np.concatenate([i["L0_ffn_shared_down_w"][None], i["L0_ffn_experts_down"]])
    dn = np.ascontiguousarray(dn.transpose(1, 0, 2))
    return {"x": i["x"], "ctxT": ctxT, "inwT": inwT, "taps": taps, "small": np.ascontiguousarray(small), "gu": gu, "dn": dn}


def kernel(**inputs):
    import concourse.bacc as _bacc
    from concourse.bass_utils import run_bass_kernel_spmd as _run

    nc = _bacc.Bacc("TRN2", target_bir_lowering=False, num_devices=1)
    arrays, args = {}, []
    for name, a in lay_out({k: np.asarray(v) for k, v in inputs.items()}).items():
        a = np.ascontiguousarray(a)
        arrays[f"in_{name}_dram"] = a
        args.append(nc.dram_tensor(f"in_{name}_dram", a.shape, mybir.dt.from_np(a.dtype), kind="ExternalInput").ap())
    args.append(nc.dram_tensor("out_0_dram", inputs["x"].shape, F32, kind="ExternalOutput").ap())
    block_kernel(nc, *args)
    r = _run(nc, [arrays], core_ids=[0])
    return r.results[0]["out_0_dram"]
```
